# Optimizing a Trainium2 kernel written in Bass

```python
import numpy as np
import jax
import jax.numpy as jnp

def _softmax(x, axis=-1):
    return jax.nn.softmax(x, axis=axis)

def _gelu(x):
    return jax.nn.gelu(x, approximate=True)

def _silu(x):
    return jax.nn.silu(x)

def _sigmoid(x):
    return jax.nn.sigmoid(x)

def _layernorm(x, axis=-1, eps=1e-05):
    m = jnp.mean(x, axis=axis, keepdims=True)
    v = jnp.var(x, axis=axis, keepdims=True)
    return (x - m) / jnp.sqrt(v + eps)

def _scatter_add(tgt, idx, src, axis=0):
    return tgt.at[idx].add(src)

def _segment_sum(src, seg, n):
    return jax.ops.segment_sum(src, seg, n)
kernel_name = 'mk_audio_tower_d1_tok_audfeat2048_r4_aa2db9'

def setup_inputs(seed: int=0):
    np.random.seed(seed)
    _w = jnp.asarray

    def _rec_inputs():
        import jax
        import jax.numpy as jnp
        _rk = jax.random.key(seed)
        x = -0.000520686 + 1.00062 * jax.random.normal(jax.random.fold_in(_rk, 1), (64, 750, 1), jnp.float32)
        return x
    x = _rec_inputs()

    def _L0_tok_setup():
        import jax, jax.numpy as jnp
        import numpy as np
        PATCH_LEN = 128
        D_MODEL = 512
        BATCH = 128
        SEQ_LEN = 4096
        FEATURES = 1
        key = jax.random.key(seed)
        k1, k2, k3 = jax.random.split(key, 3)
        x = jax.random.normal(k1, (BATCH, SEQ_LEN, FEATURES), dtype=jnp.float32)
        W = jax.random.normal(k2, (D_MODEL, PATCH_LEN), dtype=jnp.float32) * (1.0 / np.sqrt(PATCH_LEN))
        b = jax.random.normal(k3, (D_MODEL,), dtype=jnp.float32) * 0.01
        return {'x': x, 'W': W, 'b': b}
    _L0_tok_all = _L0_tok_setup()
    _L0_tok_in = {k: v for k, v in _L0_tok_all.items() if k in ('W', 'b')}
    del _L0_tok_all

    def _L0_attn_setup():
        import jax, jax.numpy as jnp
        import numpy as np
        import math
        NUM_HEADS = 16
        HEAVY_RATIO = 0.1
        RECENT_RATIO = 0.1
        ROPE_THETA = 10000.0

        def _rotate_half(x):
            d = x.shape[-1]
            return jnp.concatenate([-x[..., d // 2:], x[..., :d // 2]], axis=-1)

        def _rope(q, k, seq_len, head_dim, dtype):
            inv_freq = 1.0 / ROPE_THETA ** (jnp.arange(0, head_dim, 2, dtype=jnp.float32) / head_dim)
            pos = jnp.arange(seq_len, dtype=jnp.float32)
            freqs = pos[:, None] * inv_freq[None, :]
            emb = jnp.concatenate([freqs, freqs], axis=-1)
            cos = jnp.cos(emb).astype(dtype)[None, None]
            sin = jnp.sin(emb).astype(dtype)[None, None]
            q = q * cos + _rotate_half(q) * sin
            k = k * cos + _rotate_half(k) * sin
            return (q, k)
        key = jax.random.key(seed)
        ks = jax.random.split(key, 5)
        b, s, h = (1, 512, 512)
        return {'hidden_states': jax.random.normal(ks[0], (b, s, h), dtype=jnp.float32), 'Wq': jax.random.normal(ks[1], (h, h), dtype=jnp.float32) * 0.02, 'Wk': jax.random.normal(ks[2], (h, h), dtype=jnp.float32) * 0.02, 'Wv': jax.random.normal(ks[3], (h, h), dtype=jnp.float32) * 0.02, 'Wo': jax.random.normal(ks[4], (h, h), dtype=jnp.float32) * 0.02}
    _L0_attn_all = _L0_attn_setup()
    _L0_attn_in = {k: v for k, v in _L0_attn_all.items() if k in ('Wq', 'Wk', 'Wv', 'Wo')}
    del _L0_attn_all

    def _L0_ffn_setup():
        import jax, jax.numpy as jnp
        import numpy as np
        HIDDEN = 512
        INTER = 2048
        BATCH, LOCAL_SEQ = (2, 1024)
        key = jax.random.key(seed)
        k1, k2, k3 = jax.random.split(key, 3)
        h_shard = jax.random.normal(k1, (BATCH, LOCAL_SEQ, HIDDEN), dtype=jnp.float32)
        w_gate_up = jax.random.normal(k2, (2 * INTER, HIDDEN), dtype=jnp.float32) * 0.02
        w_down = jax.random.normal(k3, (HIDDEN, INTER), dtype=jnp.float32) * 0.02
        return {'h_shard': h_shard, 'w_gate_up': w_gate_up, 'w_down': w_down}
    _L0_ffn_all = _L0_ffn_setup()
    _L0_ffn_in = {k: v for k, v in _L0_ffn_all.items() if k in ('w_gate_up', 'w_down')}
    del _L0_ffn_all
    return {'x': x, 'L0_tok_W': _L0_tok_in['W'], 'L0_tok_b': _L0_tok_in['b'], 'L0_attn_Wq': _L0_attn_in['Wq'], 'L0_attn_Wk': _L0_attn_in['Wk'], 'L0_attn_Wv': _L0_attn_in['Wv'], 'L0_attn_Wo': _L0_attn_in['Wo'], 'L0_ffn_w_gate_up': _L0_ffn_in['w_gate_up'], 'L0_ffn_w_down': _L0_ffn_in['w_down']}

def reference(x, L0_tok_W, L0_tok_b, L0_attn_Wq, L0_attn_Wk, L0_attn_Wv, L0_attn_Wo, L0_ffn_w_gate_up, L0_ffn_w_down):
    import jax
    import jax.numpy as jnp

    def _L0_tok_ref(x, W, b):
        import jax, jax.numpy as jnp
        import numpy as np
        PATCH_LEN = 128
        D_MODEL = 512
        BATCH = 128
        SEQ_LEN = 4096
        FEATURES = 1
        B, S, F = x.shape
        P = PATCH_LEN
        stride = P // 2
        starts = jnp.arange(0, S - P + 1, stride)
        idx = starts[:, None] + jnp.arange(P)
        patches = x[:, idx, :].reshape(B, starts.shape[0], P * F)
        patches = patches[:, :, :P]
        return jnp.einsum('bnp,dp->bnd', patches, W) + b

    def _L0_attn_ref(hidden_states, Wq, Wk, Wv, Wo):
        import jax, jax.numpy as jnp
        import numpy as np
        import math
        NUM_HEADS = 16
        HEAVY_RATIO = 0.1
        RECENT_RATIO = 0.1
        ROPE_THETA = 10000.0

        def _rotate_half(x):
            d = x.shape[-1]
            return jnp.concatenate([-x[..., d // 2:], x[..., :d // 2]], axis=-1)

        def _rope(q, k, seq_len, head_dim, dtype):
            inv_freq = 1.0 / ROPE_THETA ** (jnp.arange(0, head_dim, 2, dtype=jnp.float32) / head_dim)
            pos = jnp.arange(seq_len, dtype=jnp.float32)
            freqs = pos[:, None] * inv_freq[None, :]
            emb = jnp.concatenate([freqs, freqs], axis=-1)
            cos = jnp.cos(emb).astype(dtype)[None, None]
            sin = jnp.sin(emb).astype(dtype)[None, None]
            q = q * cos + _rotate_half(q) * sin
            k = k * cos + _rotate_half(k) * sin
            return (q, k)
        b, s, hidden = hidden_states.shape
        H = NUM_HEADS
        d = hidden // H

        def proj(W):
            return (hidden_states @ W.T).reshape(b, s, H, d).transpose(0, 2, 1, 3)
        q, k, v = (proj(Wq), proj(Wk), proj(Wv))
        q, k = _rope(q, k, s, d, hidden_states.dtype)
        scores = jnp.einsum('bhqd,bhkd->bhqk', q, k) / math.sqrt(d)
        neg = jnp.finfo(scores.dtype).min
        i = jnp.arange(s)[:, None]
        j = jnp.arange(s)[None, :]
        causal = jnp.where(j <= i, jnp.array(0.0, scores.dtype), neg)
        scores = jnp.maximum(scores + causal, neg)
        heavy_budget = int(HEAVY_RATIO * s)
        recent_budget = int(RECENT_RATIO * s)
        tmp_attn = jax.nn.softmax(scores.astype(jnp.float32), axis=-1).astype(scores.dtype)
        tmp_sum = jnp.sum(tmp_attn, axis=-2)
        _, topk_idx = jax.lax.top_k(tmp_sum, heavy_budget)
        heavy_mask = jnp.any(topk_idx[..., :, None] == jnp.arange(s)[None, None, None, :], axis=-2)
        band = jnp.abs(i - j) <= recent_budget
        mask = heavy_mask[:, :, None, :] | band[None, None]
        scores = jnp.where(mask, scores, neg)
        probs = jax.nn.softmax(scores.astype(jnp.float32), axis=-1).astype(q.dtype)
        attn = jnp.einsum('bhqk,bhkd->bhqd', probs, v)
        attn = attn.transpose(0, 2, 1, 3).reshape(b, s, hidden)
        return attn @ Wo.T

    def _L0_ffn_ref(h_shard, w_gate_up, w_down):
        import jax, jax.numpy as jnp
        import numpy as np
        HIDDEN = 512
        INTER = 2048
        BATCH, LOCAL_SEQ = (2, 1024)
        batch, local_seq, hidden = h_shard.shape
        gate_up = jnp.einsum('bsh,oh->bso', h_shard, w_gate_up)
        gate, up = jnp.split(gate_up, 2, axis=-1)
        h = jax.nn.silu(gate) * up
        out = jnp.einsum('bsi,hi->bsh', h, w_down)
        return out
    h = _L0_tok_ref(x, L0_tok_W, L0_tok_b)
    h = h + _L0_attn_ref(_layernorm(h, axis=-1), L0_attn_Wq, L0_attn_Wk, L0_attn_Wv, L0_attn_Wo)
    h = h + _L0_ffn_ref(_layernorm(h, axis=-1), L0_ffn_w_gate_up, L0_ffn_w_down)
    return h

_drawn_inputs = setup_inputs


def setup_inputs(seed=0):
    import zlib

    import numpy as np

    out = dict(_drawn_inputs(seed))
    spreads = {}
    factors = {'L0_tok_b': 5.564, 'L0_attn_Wq': 3.09, 'L0_attn_Wk': 3.075}
    for name, (base, spread) in spreads.items():
        noise = np.random.default_rng([zlib.crc32(name.encode()), seed]).standard_normal(out[name].shape)
        drawn = base * np.exp(spread * noise) if base else spread * noise
        out[name] = jnp.asarray(drawn.astype(out[name].dtype))
    for name, factor in factors.items():
        out[name] = (out[name] * factor).astype(out[name].dtype)
    return out
```

```python
from contextlib import ExitStack

import concourse.bass as bass
from concourse import mybir

F32 = mybir.dt.float32
F32R = mybir.dt.float32r
ALU = mybir.AluOpType
ACT = mybir.ActivationFunctionType
AX_X = mybir.AxisListType.X

P = 128
B, SEQ = 64, 750
PATCH, STRIDE = 128, 64
NPOS = len(range(0, SEQ - PATCH + 1, STRIDE))
TOK = NPOS * B
NT = TOK // P
D, H, HD = 512, 16, 32
KT = D // P
HALF = TOK // 2
G, HG = 2, 8
HJ = HG * NPOS
INTER = 2048
NB = INTER // P
EPS = 1e-5
BIG = 3.4028234663852886e38
CUTS = {"ident": P, "pair": P, "headsum": HG, "cosk": NPOS, "sink": NPOS, "cosq": NPOS, "sinq": NPOS,
        "causal": NT * NPOS, "band": NT * NPOS, "rank": NPOS}
CONSTS = sum(CUTS.values())
QK_BANK = [[0, 2, 4, 6], [6, 0, 2, 6]]
V_BANK = [0, 1, 2, 3, 0]
S_BANK = [4, 5]
PV_BANK = [0, 2, 6, 0]
WO_BANK = [2, 3, 4, 5, 2]
LN_BANK = [[5, 6, 7, 5, 6], [6, 7, 0, 1, 0]]
GATE_A, UP_A, GATE_B, UP_B = 5, 6, 7, 5


def audio_tower(nc, patches, w_tok, b_tok, w_qk, w_v, w_o, w_ffn, consts, out):
    ctx = ExitStack()
    with ctx:
        def sb(name, shape, dt=F32, stack=ctx):
            return stack.enter_context(nc.sbuf_tensor(name, shape, dt))

        def sem(name):
            return ctx.enter_context(nc.semaphore(name))

        def f32(ap):
            return ap.bitcast(F32)

        ps = ctx.enter_context(nc.psum_tensor("ps", [P, 8, 512], F32))
        ps_flat = ps[:, :, :].rearrange("p b n -> p (b n)")

        const = sb("const", [P, CONSTS])
        at, cut = 0, {}
        for name, width in CUTS.items():
            cut[name] = const[:, at:at + width]
            at += width
        bias = sb("bias", [P, D])
        stage = sb("stage", [P, 4, 2048])
        wtok_raw = sb("wtok_raw", [P, D])
        wtok = sb("wtok", [P, 2, D], F32R)
        wqk = sb("wqk", [P, 2, 4, KT, P], F32R)
        wvo = sb("wvo", [P, 2, KT, D], F32R)
        wgu = sb("wgu", [P, 2, 2, 2 * KT * P], F32R)
        wd = sb("wd", [P, 2, 2, D], F32R)
        xT = sb("xT", [P, 2, KT, TOK], F32R)
        h = sb("h", [P, NT, D])
        xn = sb("xn", [P, 2, D])
        stats = sb("stats", [P, NT, 6])
        mv = sb("mv", [P, NT, 2])
        var = sb("var", [P, NT, 1])
        neghalf = sb("neghalf", [P, 1])
        rs0 = sb("rs0", [P, NT, 1])
        rs1 = sb("rs1", [P, NT, 1])
        rs2 = sb("rs2", [P, NT, 1])
        rstd = sb("rstd", [P, NT, 1])
        attn_mem = ExitStack()
        pat_raw = sb("pat_raw", [P, TOK], F32, attn_mem)
        pat = sb("pat", [P, 2, TOK], F32R, attn_mem)
        qk = sb("qk", [P, 4, TOK], F32, attn_mem)
        blk = sb("blk", [P, NT * (NT + 1) * 256], F32, attn_mem)
        v = sb("v", [P, NPOS, D], F32, attn_mem)
        sm = sb("sm", [P, NT, HG, NPOS], F32, attn_mem)
        ex = sb("ex", [P, NT, HG, NPOS], F32, attn_mem)
        pr = sb("pr", [P, NT, HG, NPOS], F32, attn_mem)
        keep = sb("keep", [P, NT, HG, NPOS], F32, attn_mem)
        rowv = sb("rowv", [P, 2, NT, HG], F32, attn_mem)
        hvy = sb("hvy", [P, 3, HG, NPOS], F32, attn_mem)
        hvm = sb("hvm", [P, 2, HG], F32, attn_mem)
        attn_mem.close()
        silu = sb("silu", [P, 2, HALF])
        gu = sb("gu", [P, 2, HALF])
        hT = sb("hT", [P, 2, 2, TOK], F32R)
        ob = sb("ob", [P, NT, D])

        dma_pat, dma_tok, dma_bias, dma_const = sem("dma_pat"), sem("dma_tok"), sem("dma_bias"), sem("dma_const")
        dma_stage = [sem(f"dma_stage{n}") for n in range(4)]
        dma_vdup, dma_out = sem("dma_vdup"), sem("dma_out")
        pat_hi, pat_lo, wtok_hi, wtok_lo = sem("pat_hi"), sem("pat_lo"), sem("wtok_hi"), sem("wtok_lo")
        wqk_hi, wqk_lo, wvo_hi, wvo_lo = sem("wqk_hi"), sem("wqk_lo"), sem("wvo_hi"), sem("wvo_lo")
        wgu_hi, wgu_lo, wd_hi, wd_lo = sem("wgu_hi"), sem("wgu_lo"), sem("wd_hi"), sem("wd_lo")
        tok_mm, ln_mv, ln_pow, xn_ready = sem("tok_mm"), sem("ln_mv"), sem("ln_pow"), sem("xn_ready")
        xnT_mm, xT_hi, xT_lo = sem("xnT_mm"), sem("xT_hi"), sem("xT_lo")
        qk_mm, rope_read, rope_k, k_ready = sem("qk_mm"), sem("rope_read"), sem("rope_k"), sem("k_ready")
        v_mm, v_sb = sem("v_mm"), sem("v_sb")
        prod_ready, s_mm, exp_in, exp_out = sem("prod_ready"), sem("s_mm"), sem("exp_in"), sem("exp_out")
        attn1_ready, heavy_mm, pv_ready, pv_mm = sem("attn1_ready"), sem("heavy_mm"), sem("pv_ready"), sem("pv_mm")
        attn_hi, attn_lo, wo_mm = sem("attn_hi"), sem("attn_lo"), sem("wo_mm")
        gu_mm, silu_done, gu_prod, hT_hi, hT_lo = sem("gu_mm"), sem("silu_done"), sem("gu_prod"), sem("hT_hi"), sem("hT_lo")
        down_mm, out_sb = sem("down_mm"), sem("out_sb")
        dve_step, pool_step = sem("dve_step"), sem("pool_step")

        def repeated(ap, dim, n):
            ap = ap.unsqueeze(dim)
            return ap.broadcast_to([n if d == dim else size for d, size in enumerate(ap.shape)])

        def slot(t):
            return blk[:, 256 * t * (t + 1):256 * (t + 1) * (t + 2)]

        def mm3(pe, dst, lhs, rhs, first, last):
            for n, (a, b) in enumerate(((0, 0), (0, 1), (1, 0))):
                ins = pe.matmul(dst, lhs[a], rhs[b], start=first and n == 0, stop=last and n == 2)
            return ins

        block = ctx.enter_context(nc.Block())

        @block.sync
        def _(sp):
            sp.dma_start(pat_raw[:, :], patches).then_inc(dma_pat, 16)
            sp.dma_start(wtok_raw[:, :], w_tok).then_inc(dma_tok, 16)
            sp.dma_start(bias[:, :], b_tok.partition_broadcast(P)).then_inc(dma_bias, 16)
            sp.dma_start(stage[:, 0, :], w_qk[0]).then_inc(dma_stage[0], 16)
            sp.dma_start(const[:, :], consts).then_inc(dma_const, 16)
            sp.dma_start(stage[:, 2, :], w_v).then_inc(dma_stage[2], 16)
            sp.dma_start(stage[:, 1, :], w_qk[1]).then_inc(dma_stage[1], 16)
            sp.dma_start(stage[:, 3, :], w_o).then_inc(dma_stage[3], 16)
            sp.wait_ge(v_sb, 2 * NT)
            sp.dma_start(v[B:P, 0:NPOS:2, :], v[0:B, 0:NPOS:2, :]).then_inc(dma_vdup, 16)
            sp.dma_start(v[0:B, 1:NPOS:2, :], v[B:P, 1:NPOS:2, :]).then_inc(dma_vdup, 16)
            for i in range(2):
                sp.wait_ge(wqk_hi, 4 * (i + 1))
                sp.wait_ge(wqk_lo, 4 * (i + 1))
                sp.dma_start(stage[:, i, 0:1536], w_ffn[i]).then_inc(dma_stage[i], 16)
            with sp.Fori(0, NB // 2 - 1) as n:
                for u in range(2):
                    sp.wait_ge(wgu_hi, 2 * n + (u + 1))
                    sp.wait_ge(wgu_lo, 2 * n + (u + 1))
                    sp.wait_ge(wd_hi, 2 * n + (u + 1))
                    sp.wait_ge(wd_lo, 2 * n + (u + 1))
                    sp.dma_start(stage[:, u, 0:1536], w_ffn[bass.ds(2 * n + (u + 2), 1)].rearrange("o p n -> (o p) n"))\
                      .then_inc(dma_stage[u], 16)
            for t in range(NT):
                sp.wait_ge(out_sb, t + 1)
                for par in range(2):
                    sp.dma_start(out[:, 2 * t + par, :], ob[B * par:B * (par + 1), t, :]).then_inc(dma_out, 16)
            sp.wait_ge(dma_out, 16 * 2 * NT)

        @block.gpsimd
        def _(pool):
            def lo_qk(g, m):
                pool.wait_ge(wqk_hi, 4 * g + m + 1)
                pool.tensor_tensor(wqk[:, 1, m].rearrange("p k n -> p (k n)"), stage[:, g, 512 * m:512 * (m + 1)],
                                   f32(wqk[:, 0, m].rearrange("p k n -> p (k n)")), ALU.subtract).then_inc(wqk_lo, 1)

            def lo_vo(n, k):
                pool.wait_ge(wvo_hi, KT * n + k + 1)
                pool.tensor_tensor(wvo[:, 1, k], stage[:, 2 + n, 512 * k:512 * (k + 1)], f32(wvo[:, 0, k]),
                                   ALU.subtract).then_inc(wvo_lo, 1)

            def powers(ln):
                for t in range(NT):
                    pool.wait_ge(ln_mv, NT * ln + t + 1)
                    pool.tensor_scalar(var[:, t], mv[:, t, 1:2], EPS, None, ALU.add).then_inc(pool_step, 1)
                    pool.wait_ge(pool_step, NT * ln + t + 2)
                    pool.tensor_tensor(rs0[:, t], var[:, t], neghalf[:, :], ALU.pow).then_inc(ln_pow, 1)

            def rope_sums(g):
                pool.wait_ge(rope_k, g + 1)
                tmp = blk[:, 0:4 * TOK].rearrange("p (a n) -> p a n", a=4)
                pool.tensor_tensor(qk[:, 0], tmp[:, 0], tmp[:, 1], ALU.subtract).then_inc(k_ready, 1)
                pool.tensor_tensor(qk[:, 1], tmp[:, 2], tmp[:, 3], ALU.add).then_inc(k_ready, 1)

            pool.memset(neghalf[:, :], -0.5).then_inc(pool_step, 1)
            lo_qk(0, 0)
            lo_qk(0, 1)
            powers(0)
            lo_qk(0, 2)
            lo_qk(0, 3)
            for k in range(KT):
                lo_vo(0, k)
            rope_sums(0)
            for m in range(4):
                lo_qk(1, m)
            rope_sums(1)
            for k in range(KT):
                lo_vo(1, k)

            def lo_down(i, slot_i, ring):
                pool.wait_ge(wd_hi, i + 1)
                pool.tensor_tensor(wd[:, ring, 1], stage[:, slot_i, 1024:1536], f32(wd[:, ring, 0]), ALU.subtract)\
                    .then_inc(wd_lo, 1)

            lo_down(0, 0, 0)
            powers(1)
            lo_down(1, 1, 1)
            with pool.Fori(0, NB // 2 - 1) as n:
                for u in range(2):
                    lo_down(2 * n + (u + 2), u, u)

        @block.scalar
        def _(act):
            def split_hi(dst, src, done):
                act.activation(dst, src, ACT.Copy).then_inc(done, 1)

            act.wait_ge(dma_pat, 16)
            split_hi(pat[:, 0], pat_raw[:, :], pat_hi)
            act.wait_ge(dma_tok, 16)
            split_hi(wtok[:, 0], wtok_raw[:, :], wtok_hi)

            def hi_qk(g):
                act.wait_ge(dma_stage[g], 16)
                for m in range(4):
                    if g == 1:
                        act.wait_ge(qk_mm, m + 1)
                        act.wait_ge(wqk_lo, 4)
                    split_hi(wqk[:, 0, m].rearrange("p k n -> p (k n)"), stage[:, g, 512 * m:512 * (m + 1)], wqk_hi)

            def hi_vo(n):
                act.wait_ge(dma_stage[2 + n], 16)
                if n == 1:
                    act.wait_ge(v_mm, NT)
                    act.wait_ge(wvo_lo, KT)
                for k in range(KT):
                    split_hi(wvo[:, 0, k], stage[:, 2 + n, 512 * k:512 * (k + 1)], wvo_hi)

            def hi_xT(ln):
                for t in range(NT):
                    act.wait_ge(xnT_mm, NT * ln + t + 1)
                    split_hi(xT[:, 0, :, P * t:P * (t + 1)],
                             ps[:, LN_BANK[ln][t], :].rearrange("p (k n) -> p k n", k=KT), xT_hi)

            def exponential(n):
                act.wait_ge(exp_in, n + 1)
                act.activation(ex[:, :, :, :], pr[:, :, :, :], ACT.Exp).then_inc(exp_out, 1)

            def hi_attn(c):
                act.wait_ge(pv_mm, 10 * (c // 2) + 9 + c % 2)
                split_hi(xT[:, 0, c], ps_flat[:, 512 * PV_BANK[c]:512 * PV_BANK[c] + TOK], attn_hi)

            hi_qk(0)
            hi_xT(0)
            hi_vo(0)
            hi_qk(1)
            for t in range(NT):
                act.wait_ge(v_mm, t + 1)
                for par in range(2):
                    rows = slice(B * par, B * (par + 1))
                    act.activation(v[rows, 2 * t + par, :], ps[rows, V_BANK[t], :], ACT.Copy).then_inc(v_sb, 1)
            exponential(0)
            exponential(1)
            hi_vo(1)

            def hi_gu(i, slot_i, ring, landed):
                act.wait_ge(dma_stage[slot_i], landed)
                split_hi(wgu[:, ring, 0], stage[:, slot_i, 0:1024], wgu_hi)

            def hi_down(i, slot_i, ring):
                split_hi(wd[:, ring, 0], stage[:, slot_i, 1024:1536], wd_hi)

            hi_gu(0, 0, 0, 32)
            hi_down(0, 0, 0)
            hi_gu(1, 1, 1, 32)
            exponential(2)
            hi_attn(0)
            hi_attn(1)
            exponential(3)
            hi_attn(2)
            hi_attn(3)
            hi_xT(1)

            def ffn_step(i, ring, first=False, next_gu=True, next_down=True):
                for half in range(2):
                    act.wait_ge(gu_mm, 4 * i + (2 * half + 1))
                    act.activation(silu[:, half], ps[:, (GATE_A, GATE_B)[half], 0:HALF], ACT.Silu).then_inc(silu_done, 1)
                    act.wait_ge(gu_prod, 2 * i + (half + 1))
                    if not first:
                        act.wait_ge(down_mm, i - 1)
                    split_hi(hT[:, ring, 0, HALF * half:HALF * (half + 1)], gu[:, half], hT_hi)
                if next_gu:
                    act.wait_ge(gu_mm, 4 * i + 4)
                    act.wait_ge(wgu_lo, i + 1)
                    hi_gu(i + 2, ring, ring, i * 8 + (48 - 8 * ring))
                if next_down:
                    if not (isinstance(i, int) and i < 1):
                        act.wait_ge(down_mm, i)
                        act.wait_ge(wd_lo, i)
                    hi_down(i + 1, 1 - ring, 1 - ring)

            ffn_step(0, 0, first=True)
            ffn_step(1, 1, first=True)
            with act.Fori(0, NB // 2 - 2) as n:
                ffn_step(2 * n + 2, 0)
                ffn_step(2 * n + 3, 1)
            ffn_step(NB - 2, 0, next_gu=False)
            ffn_step(NB - 1, 1, next_gu=False, next_down=False)

        @block.vector
        def _(dve):
            steps = [0]

            def step(ins):
                steps[0] += 1
                ins.then_inc(dve_step, 1)
                dve.wait_ge(dve_step, steps[0])

            def layer_norm(ln, load):
                def normalise(t):
                    dve.wait_ge(ln_pow, NT * ln + t + 1)
                    step(dve.tensor_scalar(rs1[:, t], var[:, t], rs0[:, t], rs0[:, t], ALU.mult, ALU.mult))
                    step(dve.tensor_scalar(rs2[:, t], rs1[:, t], -0.5, 1.5, ALU.mult, ALU.add))
                    step(dve.tensor_tensor(rstd[:, t], rs0[:, t], rs2[:, t], ALU.mult))
                    if NT * ln + t >= 2:
                        dve.wait_ge(xnT_mm, NT * ln + t - 1)
                    dve.tensor_scalar(xn[:, (NT * ln + t) % 2], h[:, t], mv[:, t, 0:1], rstd[:, t],
                                      ALU.subtract, ALU.mult).then_inc(xn_ready, 1)

                def low(t):
                    dve.wait_ge(xT_hi, NT * ln + t + 1)
                    cols = slice(P * t, P * (t + 1))
                    dve.tensor_tensor(xT[:, 1, :, cols], ps[:, LN_BANK[ln][t], :].rearrange("p (k n) -> p k n", k=KT),
                                      f32(xT[:, 0, :, cols]), ALU.subtract).then_inc(xT_lo, 1)

                for t in range(NT + 2):
                    if t < NT:
                        step(load(t))
                        step(dve.bn_stats(stats[:, t], h[:, t]))
                        dve.bn_aggr(mv[:, t], stats[:, t]).then_inc(ln_mv, 1)
                    if 1 <= t <= NT:
                        normalise(t - 1)
                    if t >= 2:
                        low(t - 2)

            dve.wait_ge(pat_hi, 1)
            dve.tensor_tensor(pat[:, 1], pat_raw[:, :], f32(pat[:, 0]), ALU.subtract).then_inc(pat_lo, 1)
            dve.wait_ge(wtok_hi, 1)
            dve.tensor_tensor(wtok[:, 1], wtok_raw[:, :], f32(wtok[:, 0]), ALU.subtract).then_inc(wtok_lo, 1)

            def embed(t):
                dve.wait_ge(tok_mm, t + 1)
                if t == 0:
                    dve.wait_ge(dma_bias, 16)
                return dve.tensor_tensor(h[:, t], ps[:, t, :], bias[:, :], ALU.add)

            layer_norm(0, embed)
            dve.wait_ge(dma_const, 16)
            dve.memset(sm[:, :, :, :], -BIG)

            def rope(g, x):
                dve.wait_ge(qk_mm, 4 * g + 2 * x + 2)
                half = [ps[:, QK_BANK[g][2 * x + n]:QK_BANK[g][2 * x + n] + 2, 0:HALF]
                        .rearrange("p a (i b) -> p a i b", b=B) for n in range(2)]
                tmp = blk[:, 4 * TOK * x:4 * TOK * (x + 1)].rearrange("p (f a i b) -> p f a i b", f=4, a=2, b=B)
                cos, sin = (repeated(cut[n + "kq"[x]].rearrange("p (a i) -> p a i", a=2), 3, B) for n in ("cos", "sin"))
                for f, (n, table) in enumerate(((0, cos), (1, sin), (1, cos), (0, sin))):
                    last = dve.tensor_tensor(tmp[:, f], half[n], table, ALU.mult)
                if x == 0:
                    last.then_inc(rope_k, 1)
                    return
                last.then_inc(rope_read, 1)
                dve.wait_ge(rope_read, g + 1)
                flat = blk[:, 4 * TOK:8 * TOK].rearrange("p (f n) -> p f n", f=4)
                dve.tensor_tensor(qk[:, 2], flat[:, 0], flat[:, 1], ALU.subtract)
                step(dve.tensor_tensor(qk[:, 3], flat[:, 2], flat[:, 3], ALU.add))

            def products(g):
                dve.wait_ge(k_ready, 2 * (g + 1))
                for t in range(NT):
                    nj = 2 * t + 2
                    dst = slot(t).rearrange("p (s j a b) -> p s j a b", s=2, j=nj, b=B)
                    for s in range(2):
                        q = repeated(qk[:, 2 + s, P * t:P * (t + 1)].rearrange("p (a b) -> p a b", b=B), 1, nj)
                        k = repeated(qk[:, s, 0:B * nj].rearrange("p (j b) -> p j b", b=B), 2, 2)
                        last = dve.tensor_tensor(dst[:, s], q, k, ALU.mult)
                    last.then_inc(prod_ready, 1)

            rows40 = [rowv[:, n].rearrange("p t h -> p (t h)") for n in range(2)]

            def flat3(x):
                return x[:, :, :, :].rearrange("p t h j -> p (t h) j")

            def spread(x):
                return repeated(x, 2, NPOS)

            def softmax_in(n):
                step(dve.tensor_reduce(rows40[0], flat3(sm), AX_X, ALU.max))
                dve.tensor_tensor(flat3(pr), flat3(sm), spread(rows40[0]), ALU.subtract).then_inc(exp_in, 1)

            def softmax_out(n):
                dve.wait_ge(exp_out, n + 1)
                step(dve.tensor_reduce(rows40[0], flat3(ex), AX_X, ALU.add))
                step(dve.reciprocal(rows40[1], rows40[0]))
                return dve.tensor_tensor(flat3(pr), flat3(ex), spread(rows40[1]), ALU.mult)

            def first_softmax(g):
                dve.wait_ge(s_mm, NT * (g + 1))
                for t in range(NT):
                    nj = 2 * t + 2
                    scores = ps[:, S_BANK[g], HJ * t:HJ * t + HG * nj].rearrange("p (j h) -> p h j", h=HG)
                    mask = repeated(cut["causal"][:, NPOS * t:NPOS * t + nj], 1, HG)
                    last = dve.scalar_tensor_tensor(sm[:, t, :, 0:nj], scores, -BIG, mask, ALU.max, ALU.min)
                step(last)
                softmax_in(2 * g)
                softmax_out(2 * g).then_inc(attn1_ready, 1)

            def second_softmax(g):
                dve.wait_ge(heavy_mm, g + 1)
                total = ps[:, S_BANK[g], NT * HJ:NT * HJ + HJ].rearrange("p (h j) -> p h j", h=HG)
                step(dve.tensor_reduce(hvm[:, 0], total, AX_X, ALU.max))
                step(dve.tensor_tensor(hvy[:, 0], total, spread(hvm[:, 0]), ALU.is_equal))
                step(dve.tensor_tensor(hvy[:, 1], hvy[:, 0], repeated(cut["rank"], 1, HG), ALU.mult))
                step(dve.tensor_reduce(hvm[:, 1], hvy[:, 1], AX_X, ALU.max))
                step(dve.tensor_tensor(hvy[:, 2], hvy[:, 1], spread(hvm[:, 1]), ALU.is_equal))
                step(dve.tensor_scalar(hvy[:, 0], hvy[:, 2], 2.0, -1.0, ALU.mult, ALU.add))
                step(dve.tensor_scalar(hvy[:, 1], hvy[:, 0], BIG, None, ALU.mult))
                step(dve.tensor_tensor(keep[:, :, :, :], repeated(hvy[:, 1], 1, NT),
                                       repeated(cut["band"].rearrange("p (t j) -> p t j", t=NT), 2, HG),
                                       ALU.max))
                step(dve.tensor_tensor(flat3(sm), flat3(sm), flat3(keep), ALU.min))
                softmax_in(2 * g + 1)
                step(softmax_out(2 * g + 1))

            def weighted_values(g):
                if g == 0:
                    dve.wait_ge(dma_vdup, 32)
                for t in range(NT):
                    nj = 2 * t + 2
                    if g == 0:
                        dve.wait_ge(s_mm, NT + t + 1)
                    else:
                        dve.wait_ge(pv_mm, 2 * t + 2)
                    dst = slot(t).rearrange("p (j h d) -> p j h d", j=nj, h=HG)
                    vals = v[:, 0:nj, 256 * g:256 * (g + 1)].rearrange("p j (h d) -> p j h d", h=HG)
                    prob = repeated(pr[:, t, :, 0:nj].rearrange("p h j -> p j h"), 3, HD)
                    dve.tensor_tensor(dst, vals, prob, ALU.mult).then_inc(pv_ready, 1)

            def low_attn(c):
                dve.wait_ge(attn_hi, c + 1)
                dve.tensor_tensor(xT[:, 1, c], ps_flat[:, 512 * PV_BANK[c]:512 * PV_BANK[c] + TOK], f32(xT[:, 0, c]),
                                  ALU.subtract).then_inc(attn_lo, 1)

            def lo_gu(i, slot_i, ring):
                dve.wait_ge(wgu_hi, i + 1)
                dve.tensor_tensor(wgu[:, ring, 1], stage[:, slot_i, 0:1024], f32(wgu[:, ring, 0]), ALU.subtract)\
                   .then_inc(wgu_lo, 1)

            rope(0, 0)
            rope(0, 1)
            products(0)
            first_softmax(0)
            second_softmax(0)
            rope(1, 0)
            rope(1, 1)
            products(1)
            weighted_values(0)
            first_softmax(1)
            lo_gu(0, 0, 0)
            lo_gu(1, 1, 1)
            low_attn(0)
            low_attn(1)
            second_softmax(1)
            weighted_values(1)
            low_attn(2)
            low_attn(3)

            def add_attention(t):
                dve.wait_ge(wo_mm, t + 1)
                return dve.tensor_tensor(h[:, t], ps[:, WO_BANK[t], :], h[:, t], ALU.add)

            layer_norm(1, add_attention)

            def ffn_step(i, ring, next_gu=True):
                for half in range(2):
                    dve.wait_ge(gu_mm, 4 * i + (2 * half + 2))
                    dve.wait_ge(silu_done, 2 * i + (half + 1))
                    dve.tensor_tensor(gu[:, half], silu[:, half], ps[:, (UP_A, UP_B)[half], 0:HALF], ALU.mult)\
                       .then_inc(gu_prod, 1)
                    dve.wait_ge(hT_hi, 2 * i + (half + 1))
                    cols = slice(HALF * half, HALF * (half + 1))
                    dve.tensor_tensor(hT[:, ring, 1, cols], gu[:, half], f32(hT[:, ring, 0, cols]), ALU.subtract)\
                       .then_inc(hT_lo, 1)
                if next_gu:
                    lo_gu(i + 2, ring, ring)

            ffn_step(0, 0)
            ffn_step(1, 1)
            with dve.Fori(0, NB // 2 - 2) as n:
                ffn_step(2 * n + 2, 0)
                ffn_step(2 * n + 3, 1)
            ffn_step(NB - 2, 0, next_gu=False)
            ffn_step(NB - 1, 1, next_gu=False)
            for t in range(NT):
                dve.wait_ge(down_mm, NB - 1 + t + 1)
                dve.tensor_tensor(ob[:, t], ps[:, t, :], h[:, t], ALU.add).then_inc(out_sb, 1)

        @block.tensor
        def _(pe):
            for s in (pat_hi, pat_lo, wtok_hi, wtok_lo):
                pe.wait_ge(s, 1)
            for t in range(NT):
                mm3(pe, ps[:, t, :], [pat[:, a, P * t:P * (t + 1)] for a in range(2)],
                    [wtok[:, a] for a in range(2)], True, True).then_inc(tok_mm, 1)

            def transposes(ln):
                if ln == 0:
                    pe.wait_ge(dma_const, 16)
                for t in range(NT):
                    pe.wait_ge(xn_ready, NT * ln + t + 1)
                    again = [u for u in range(t) if LN_BANK[ln][u] == LN_BANK[ln][t]]
                    if again:
                        pe.wait_ge(xT_lo, NT * ln + again[-1] + 1)
                    for k in range(KT):
                        ins = pe.transpose(ps[:, LN_BANK[ln][t], P * k:P * (k + 1)],
                                           xn[:, (NT * ln + t) % 2, P * k:P * (k + 1)], cut["ident"])
                    ins.then_inc(xnT_mm, 1)

            def project_qk(g, m):
                pe.wait_ge(wqk_hi, 4 * g + m + 1)
                pe.wait_ge(wqk_lo, 4 * g + m + 1)
                for half in range(2):
                    if g == 0 and m == 0:
                        pe.wait_ge(xT_lo, (3, NT)[half])
                    for k in range(KT):
                        ins = mm3(pe, ps[:, QK_BANK[g][m] + half, 0:HALF], [wqk[:, a, m, k] for a in range(2)],
                                  [xT[:, a, k, HALF * half:HALF * (half + 1)] for a in range(2)], k == 0, k == KT - 1)
                ins.then_inc(qk_mm, 1)

            def project_v():
                pe.wait_ge(rope_k, 1)
                for t in range(NT):
                    if t == NT - 1:
                        pe.wait_ge(v_sb, 2)
                    for k in range(KT):
                        if t == 0:
                            pe.wait_ge(wvo_lo, k + 1)
                        ins = mm3(pe, ps[:, V_BANK[t], :], [xT[:, a, k, P * t:P * (t + 1)] for a in range(2)],
                                  [wvo[:, a, k] for a in range(2)], k == 0, k == KT - 1)
                    ins.then_inc(v_mm, 1)

            def head_sums(g):
                for t in range(NT):
                    pe.wait_ge(prod_ready, NT * g + t + 1)
                    nj = 2 * t + 2
                    src = slot(t).rearrange("p (s j n) -> p s j n", s=2, j=nj)
                    for j in range(nj):
                        for s in range(2):
                            ins = pe.matmul(ps[:, S_BANK[g], HJ * t + HG * j:HJ * t + HG * (j + 1)], src[:, s, j],
                                            cut["headsum"], start=s == 0, stop=s == 1)
                    ins.then_inc(s_mm, 1)

            def query_sums(g):
                pe.wait_ge(attn1_ready, g + 1)
                for t in range(NT):
                    ins = pe.matmul(ps[:, S_BANK[g], NT * HJ:NT * HJ + HJ], cut["pair"],
                                    pr[:, t].rearrange("p h j -> p (h j)"), start=t == 0, stop=t == NT - 1)
                ins.then_inc(heavy_mm, 1)

            def value_sums(g):
                for t in range(NT):
                    pe.wait_ge(pv_ready, NT * g + t + 1)
                    nj = 2 * t + 2
                    src = slot(t).rearrange("p (j n) -> p j n", j=nj)
                    for c in range(2):
                        at = 512 * PV_BANK[2 * g + c] + P * t
                        if g == 1 and c == 1 and t == 0:
                            pe.wait_ge(attn_lo, 1)
                        for j in range(nj):
                            ins = pe.matmul(ps_flat[:, at:at + P], src[:, j, P * c:P * (c + 1)], cut["ident"],
                                            start=j == 0, stop=j == nj - 1)
                        ins.then_inc(pv_mm, 1)

            transposes(0)
            for m in range(4):
                project_qk(0, m)
            project_v()
            pe.wait_ge(rope_read, 1)
            head_sums(0)
            project_qk(1, 0)
            query_sums(0)
            pe.wait_ge(v_sb, 2 * NT)
            project_qk(1, 1)
            project_qk(1, 2)
            pe.wait_ge(rope_k, 2)
            project_qk(1, 3)
            head_sums(1)
            value_sums(0)
            query_sums(1)
            value_sums(1)
            pe.wait_ge(attn_lo, 4)
            pe.wait_ge(wvo_lo, 2 * KT)
            for t in range(NT):
                if t == NT - 1:
                    pe.wait_ge(ln_mv, NT + 1)
                for k in range(KT):
                    ins = mm3(pe, ps[:, WO_BANK[t], :], [xT[:, a, k, P * t:P * (t + 1)] for a in range(2)],
                              [wvo[:, a, k] for a in range(2)], k == 0, k == KT - 1)
                ins.then_inc(wo_mm, 1)
            transposes(1)

            def gate_up(i, ring, first=False):
                pe.wait_ge(wgu_lo, i + 1)
                if first:
                    pe.wait_ge(ln_mv, 2 * NT)
                else:
                    pe.wait_ge(gu_prod, 2 * i)
                for half in range(2):
                    if first:
                        pe.wait_ge(xT_lo, NT + (3, NT)[half])
                    for up, bank in enumerate(((GATE_A, UP_A), (GATE_B, UP_B))[half]):
                        if half and up:
                            pe.wait_ge(silu_done, 2 * i + 1)
                        for k in range(KT):
                            at = 512 * up + P * k
                            ins = mm3(pe, ps[:, bank, 0:HALF], [wgu[:, ring, a, at:at + P] for a in range(2)],
                                      [xT[:, a, k, HALF * half:HALF * (half + 1)] for a in range(2)],
                                      k == 0, k == KT - 1)
                        ins.then_inc(gu_mm, 1)

            def down(i, ring, first=False, last=False):
                pe.wait_ge(hT_lo, 2 * i + 2)
                pe.wait_ge(wd_lo, i + 1)
                for t in range(NT):
                    ins = mm3(pe, ps[:, t, :], [hT[:, ring, a, P * t:P * (t + 1)] for a in range(2)],
                              [wd[:, ring, a] for a in range(2)], first, last)
                    if last:
                        ins.then_inc(down_mm, 1)
                if not last:
                    ins.then_inc(down_mm, 1)

            gate_up(0, 0, first=True)
            gate_up(1, 1)
            down(0, 0, first=True)
            with pe.Fori(0, NB // 2 - 1) as n:
                gate_up(2 * n + 2, 0)
                down(2 * n + 1, 1)
                gate_up(2 * n + 3, 1)
                down(2 * n + 2, 0)
            down(NB - 1, 1, last=True)


def lay_out(x, L0_tok_W, L0_tok_b, L0_attn_Wq, L0_attn_Wk, L0_attn_Wv, L0_attn_Wo, L0_ffn_w_gate_up, L0_ffn_w_down):
    import numpy as np

    xs = np.asarray(x)[:, :, 0]
    patches = np.stack([xs[:, STRIDE * i:STRIDE * i + PATCH].T for i in range(NPOS)], axis=1).reshape(P, TOK)

    def k_major(w):
        w = np.asarray(w)
        return w.T.reshape(-1, P, w.shape[0]).transpose(1, 0, 2)

    def rope_parts(w):
        return k_major(w).reshape(P, KT, G, HG, 2, HD // 2).transpose(0, 1, 2, 4, 3, 5).reshape(P, KT, G, 2, P)

    q, k = rope_parts(L0_attn_Wq), rope_parts(L0_attn_Wk)
    w_qk = np.concatenate([k, q], axis=3).transpose(2, 0, 3, 1, 4).reshape(G, P, 4 * KT * P)
    gate_up = k_major(L0_ffn_w_gate_up).reshape(P, KT, 2, NB, P).transpose(3, 0, 2, 1, 4).reshape(NB, P, 2 * KT * P)
    down = np.asarray(L0_ffn_w_down).T.reshape(NB, P, D)

    f = np.float32
    scale = f(1.0) / np.sqrt(f(HD))
    inv_freq = f(1.0) / f(10000.0) ** (np.arange(0, HD, 2, dtype=f) / f(HD))
    angle = (np.arange(NPOS, dtype=f)[:, None] * inv_freq[None, :]).astype(f)
    cos, sin = (np.tile(fn(angle).astype(f).T, (HG, 1)) for fn in (np.cos, np.sin))
    part = np.arange(P)
    pos = (part[:, None] // B + 2 * np.arange(NT)[None, :])[:, :, None]
    key = np.arange(NPOS)[None, None, :]
    tables = {
        "ident": np.eye(P), "pair": part[:, None] % B == part[None, :] % B,
        "headsum": part[:, None] // (HD // 2) == np.arange(HG)[None, :],
        "cosk": cos, "sink": sin, "cosq": cos * scale, "sinq": sin * scale,
        "causal": np.where(key <= pos, BIG, -BIG).reshape(P, -1),
        "band": np.where(np.abs(pos - key) <= 1, BIG, -BIG).reshape(P, -1),
        "rank": np.tile(NPOS - np.arange(NPOS), (P, 1)),
    }
    consts = np.concatenate([np.asarray(tables[n]).astype(f) for n in CUTS], axis=1)
    return {
        "patches": patches, "w_tok": np.asarray(L0_tok_W).T, "b_tok": np.asarray(L0_tok_b), "w_qk": w_qk,
        "w_v": k_major(L0_attn_Wv).reshape(P, KT * D), "w_o": k_major(L0_attn_Wo).reshape(P, KT * D),
        "w_ffn": np.concatenate([gate_up, down], axis=2), "consts": consts,
    }


def kernel(**inputs):
    import numpy as np
    from concourse import bacc
    from concourse.bass_utils import run_bass_kernel_spmd

    arrays = {n: np.ascontiguousarray(a) for n, a in lay_out(**inputs).items()}
    nc = bacc.Bacc("TRN2", target_bir_lowering=False, num_devices=1)
    args = [nc.dram_tensor(n, a.shape, F32, kind="ExternalInput").ap() for n, a in arrays.items()]
    out = nc.dram_tensor("out", (B, NPOS, D), F32, kind="ExternalOutput").ap()
    audio_tower(nc, *args, out)
    result = run_bass_kernel_spmd(nc, [arrays], core_ids=[0])
    return result.results[0]["out"]
```

```python
from contextlib import ExitStack

import concourse.bass as bass
from concourse import mybir

F32 = mybir.dt.float32
F32R = mybir.dt.float32r
ALU = mybir.AluOpType
ACT = mybir.ActivationFunctionType
AX_X = mybir.AxisListType.X

P = 128
B, SEQ = 64, 750
PATCH, STRIDE = 128, 64
NPOS = len(range(0, SEQ - PATCH + 1, STRIDE))
TOK = NPOS * B
NT = TOK // P
D, H, HD = 512, 16, 32
KT = D // P
NG, GB, NQ = 2, 32, 4
HQ = H // NQ
DH = HQ * HD
INTER = 2048
NB = INTER // P
FW = 2 * KT * P + D
EPS = 1e-5
BIG = 3.4028234663852886e38
CUTS = {"ident": P, "cosk": NT * HD, "sink": NT * HD, "cosq": NT * HD, "sinq": NT * HD,
        "band": NPOS * NPOS, "rank": NPOS}
CONSTS = sum(CUTS.values())
QUADRANTS = [[(0, n) for n in range(0, 4)], [(0, n) for n in range(4, 8)],
             [(g, n) for g in range(2) for n in (8, 9)],
             [(1, n) for n in range(0, 4)], [(1, n) for n in range(4, 8)]]

PROJECT = [("k", 0), ("q", 0), ("k", 1), ("q", 1), ("k", 2), ("q", 2), ("v", 0), ("v", 1), ("v", 2),
           ("k", 3), ("q", 3), ("k", 4), ("q", 4), ("v", 3), ("v", 4)]
ROTATE = [item for item in PROJECT if item[0] != "v"]
ROT = 4
NORMS = [(0, t) for t in range(NT)] + [(1, t) for t in (1, 0, 2, 4, 3)]
LN2 = {t: n for n, (ln, t) in enumerate(NORMS) if ln == 1}
UNITS = [(0, 1, (0, 4), (7, 6, 5, 4)), (0, 0, (0, 4), (3, 2, 1, 0)), (0, 2, (0, 2), (9, 8)),
         (1, 2, (2, 4), (9, 8)), (1, 4, (0, 4), (7, 6, 5, 4)), (1, 3, (0, 4), (3, 2, 1, 0))]
VALUES = [(unit[0], i) for unit in UNITS for i in unit[3]]
WO = [1, 0, 2, 4, 3]
POOL_SCORES = [(0, 5), (0, 7), (0, 9), (1, 5), (1, 7)]
POOL_VALUES = [(0, 9), (0, 8), (1, 8), (1, 7), (1, 4)]
SOFTMAX = [(0, 0, (0, 10)), (0, 1, (0, 8)), (0, 1, (8, 10)),
           (1, 0, (0, 10)), (1, 1, (0, 10))]
MASKED = [step for step in SOFTMAX if step[1] == 1]
LN1_BANK = [5, 6]
PROJECT_BANK = [7, 0, 1, 2, 3, 4]
UNIT_BANK = [5, 6, 2, 3, 4, 2]
WO_BANK = {1: 0, 0: 1, 2: 7, 4: 3, 3: 7}
LN2_BANK = {1: 5, 0: 6, 2: 4, 4: 2, 3: 3}
A, BB = 0, 1
FIRST, TILES = (0, 2), (2, 3)
GATE = (((5, 0), (6, 0)), ((5, 0), (7, 0)))
UP = (((5, 2 * P), (6, 2 * P)), ((6, 0), (0, 0)))
DOWN = ((0, 1), (2, 3, 4))
SLOTS = 4


def ln_bank(n):
    ln, t = NORMS[n]
    return LN2_BANK[t] if ln else LN1_BANK[n % 2]


def columns(unit):
    _, t, (a, b), _ = UNITS[unit]
    return slice(P * t + GB * a, P * t + GB * b)


def audio_tower(nc, patches, w_tok, b_tok, w_k, w_q, w_v, w_o, w_ffn, consts, regroup, out):
    ctx = ExitStack()
    with ctx:
        def sb(name, shape, dt=F32, stack=ctx):
            return stack.enter_context(nc.sbuf_tensor(name, shape, dt))

        def sem(name):
            return ctx.enter_context(nc.semaphore(name))

        def f32(ap):
            return ap.bitcast(F32)

        ps = ctx.enter_context(nc.psum_tensor("ps", [P, 8, 512], F32))

        const = sb("const", [P, CONSTS])
        at, cut = 0, {}
        for name, width in CUTS.items():
            cut[name] = const[:, at:at + width]
            at += width
        stage = sb("stage", [P, 4, 2048])
        wvo = sb("wvo", [P, 2, KT, D], F32R)
        xT = sb("xT", [P, 2, KT, TOK], F32R)
        h = sb("h", [P, NT, D])
        xn = sb("xn", [P, 2, D])
        stats = sb("stats", [P, NT, 6])
        mv = sb("mv", [P, NT, 2])
        var = sb("var", [P, NT, 1])
        neghalf = sb("neghalf", [P, 1])
        warm = sb("warm", [P, 1])
        rs0, rs1, rs2, rstd = (sb(n, [P, NT, 1]) for n in ("rs0", "rs1", "rs2", "rstd"))
        qk_mem = ExitStack()
        wkq = [sb(n, [P, 2, KT, D], F32R, qk_mem) for n in ("wk", "wq")]
        qk_mem.close()
        wgu = sb("wgu", [P, 2, 2, 2 * KT * P], F32R)
        wd = sb("wd", [P, 2, 2, D], F32R)
        ob = sb("ob", [P, 3, D])
        silu = sb("silu", [P, 2, 3 * P])
        rot_mem = ExitStack()
        rot_cos = sb("rot_cos", [P, 2, D], F32, rot_mem)
        rot_sin = sb("rot_sin", [P, 2, D], F32, rot_mem)
        rot = sb("rot", [P, ROT, D], F32, rot_mem)
        v_out = sb("v_out", [P, 2, D], F32, rot_mem)
        rot_mem.close()
        gu = sb("gu", [P, 2, 3 * P])
        hT = sb("hT", [P, 2, 2, 3 * P], F32R)
        fill = sb("fill", [P, (4 + ROT + 2) * D - 6 * P - 12 * P])
        k_all, q_all, v_all = (sb(n, [P, NG, NPOS, DH]) for n in ("k_all", "q_all", "v_all"))
        embed_mem = ExitStack()
        pat_raw = sb("pat_raw", [P, TOK], F32, embed_mem)
        pat = sb("pat", [P, 2, TOK], F32R, embed_mem)
        wtok_raw = sb("wtok_raw", [P, D], F32, embed_mem)
        wtok = sb("wtok", [P, 2, D], F32R, embed_mem)
        bias_raw = sb("bias_raw", [1, D], F32, embed_mem)
        bias = sb("bias", [1, 2, D], F32R, embed_mem)
        ones_raw = sb("ones_raw", [1, P], F32, embed_mem)
        ones = sb("ones", [1, P], F32R, embed_mem)
        embed_mem.close()
        prod = sb("prod", [P, NPOS * (NPOS + 1) // 2, DH])
        sm, pr, keep = (sb(n, [P, NPOS, HQ, NPOS]) for n in ("sm", "pr", "keep"))
        rowv = sb("rowv", [P, 2, NPOS, HQ])
        hvy = sb("hvy", [P, 3, HQ, NPOS])
        hvm = sb("hvm", [P, 2, HQ])

        dma_pat, dma_tok, dma_bias, dma_const = sem("dma_pat"), sem("dma_tok"), sem("dma_bias"), sem("dma_const")
        dma_stage = [sem(f"dma_stage{n}") for n in range(4)]
        rot_gone = [sem(f"rot_gone{n}") for n in range(ROT)]
        dma_kq = [sem(f"dma_kq{t}") for t in range(NT)]
        v_gone = [sem(f"v_gone{n}") for n in range(2)]
        dma_v = [sem(f"dma_v{g}") for g in range(NG)]
        dma_out = sem("dma_out")
        pat_hi, pat_lo, wtok_hi, wtok_lo = sem("pat_hi"), sem("pat_lo"), sem("wtok_hi"), sem("wtok_lo")
        wkq_hi, wkq_lo = [sem("wk_hi"), sem("wq_hi")], [sem("wk_lo"), sem("wq_lo")]
        wvo_hi, wvo_lo = sem("wvo_hi"), sem("wvo_lo")
        ones_set, neghalf_set = sem("ones_set"), sem("neghalf_set")
        bias_hi, bias_lo = sem("bias_hi"), sem("bias_lo")
        tok_mm, h_sb, ln_mv, ln_var, ln_pow, xn_ready = (sem(n) for n in ("tok_mm", "h_sb", "ln_mv", "ln_var", "ln_pow", "xn_ready"))
        xnT_mm, xT_hi, xT_lo = sem("xnT_mm"), sem("xT_hi"), sem("xT_lo")
        project_mm, rot_read, rot_sum, v_sb = sem("project_mm"), sem("rot_read"), sem("rot_sum"), sem("v_sb")
        score_pool, score_sum = sem("score_pool"), sem("score_sum")
        exp_in, exp_out = sem("exp_in"), sem("exp_out")
        probs, pv_dve, pv_pool, pv_mm = sem("probs"), sem("pv_dve"), sem("pv_pool"), sem("pv_mm")
        attn_hi, attn_lo, wo_mm = sem("attn_hi"), sem("attn_lo"), sem("wo_mm")
        wgu_hi, wgu_lo, wd_hi, wd_lo, gu_mm, silu_done, gu_prod, hT_hi, hT_lo, down_mm, out_sb = (
            [sem(f"{n}_{p}") for p in "ab"] for n in
            ("wgu_hi", "wgu_lo", "wd_hi", "wd_lo", "gu_mm", "silu_done", "gu_prod", "hT_hi", "hT_lo", "down_mm", "out_sb"))
        dve_step = sem("dve_step")

        def repeated(ap, dim, n):
            ap = ap.unsqueeze(dim)
            return ap.broadcast_to([n if d == dim else size for d, size in enumerate(ap.shape)])

        def mm3(pe, dst, lhs, rhs, first, last):
            for n, (a, b) in enumerate(((0, 0), (0, 1), (1, 0))):
                ins = pe.matmul(dst, lhs[a], rhs[b], start=first and n == 0, stop=last and n == 2)
            return ins

        def rotated(eng, g, i):
            for t in ((0, 1, 2), (3, 4, 2))[g][:i // 4 + 1]:
                eng.wait_ge(dma_kq[t], 16 * 2 * len({group for group, _ in QUADRANTS[t]}))

        def values_arrived(eng, g):
            eng.wait_ge(dma_v[g], 16 * 3)

        def rotation_done(eng):
            for buffer in range(ROT):
                eng.wait_ge(rot_gone[buffer], 64 * len(range(buffer, len(ROTATE), ROT)))
            for buffer in range(2):
                eng.wait_ge(v_gone[buffer], 64 * len(range(buffer, NT, 2)))

        def products(i):
            return prod[:, i * (i + 1) // 2:(i + 1) * (i + 2) // 2]

        def key_products(eng, g, i):
            if g:
                eng.wait_ge(pv_mm, VALUES.index((g - 1, i)) + 1)
            return eng.tensor_tensor(products(i), repeated(q_all[:, g, i], 1, i + 1), k_all[:, g, 0:i + 1], ALU.mult)

        def value_products(eng, g, i):
            return eng.tensor_tensor(products(i).rearrange("p j (h d) -> p j h d", d=HD),
                                     v_all[:, g, 0:i + 1].rearrange("p j (h d) -> p j h d", d=HD),
                                     repeated(pr[:, i, :, 0:i + 1].rearrange("p h j -> p j h"), 3, HD), ALU.mult)

        def value_number(item):
            return sum((k in POOL_VALUES) == (item in POOL_VALUES) for k in VALUES[:VALUES.index(item) + 1])

        def stage_count(p, i, slot):
            before = 1 + p * NB // SLOTS
            return i * (16 // SLOTS) + (16 * (before + 1) - slot * (16 // SLOTS))

        block = ctx.enter_context(nc.Block())

        @block.sync
        def _(sp):
            sp.dma_start(pat_raw[:, :], patches).then_inc(dma_pat, 16)
            sp.dma_start(wtok_raw[:, :], w_tok).then_inc(dma_tok, 16)
            sp.dma_start(bias_raw[:, :], b_tok).then_inc(dma_bias, 16)
            sp.dma_start(stage[:, 0, :], w_k).then_inc(dma_stage[0], 16)
            sp.dma_start(const[:, :], consts).then_inc(dma_const, 16)
            sp.dma_start(stage[:, 1, :], w_q).then_inc(dma_stage[1], 16)
            sp.dma_start(stage[:, 2, :], w_v).then_inc(dma_stage[2], 16)
            sp.dma_start(stage[:, 3, :], w_o).then_inc(dma_stage[3], 16)

            def leave(x, t, buffer, done):
                for q, (g, i) in enumerate(QUADRANTS[t]):
                    sp.dma_start(regroup["kqv".index(x), g, :, :, i, :].rearrange("h b n -> b h n"),
                                 buffer[GB * q:GB * (q + 1)].rearrange("p (h n) -> p h n", h=NQ)).then_inc(done, 16)

            def enter(x, t, g, done):
                dst = {"k": k_all, "q": q_all, "v": v_all}[x]
                own = [i for group, i in QUADRANTS[t] if group == g]
                at = slice(own[0], own[-1] + 1)
                sp.dma_start(dst[:, g, at, :], regroup["kqv".index(x), g].rearrange("h b i n -> (h b) i n")[:, at, :])\
                  .then_inc(done, 16)

            def pair(t):
                items = [ROTATE.index((x, t)) for x in "kq"]
                for n in items:
                    sp.wait_ge(rot_sum, n + 1)
                    leave(ROTATE[n][0], t, rot[:, n % ROT], rot_gone[n % ROT])
                for n in items:
                    sp.wait_ge(rot_gone[n % ROT], 64 * (n // ROT + 1))
                    for g in sorted({g for g, _ in QUADRANTS[t]}):
                        enter(ROTATE[n][0], t, g, dma_kq[t])

            def value_out(t):
                sp.wait_ge(v_sb, t + 1)
                leave("v", t, v_out[:, t % 2], v_gone[t % 2])

            def value_in(t):
                sp.wait_ge(v_gone[t % 2], 64 * (t // 2 + 1))
                for g in sorted({g for g, _ in QUADRANTS[t]}):
                    enter("v", t, g, dma_v[g])

            def block_load(p, i):
                slot = i % SLOTS
                sp.dma_start(stage[:, slot, 0:FW], w_ffn[i]).then_inc(dma_stage[slot], 16)

            def tile_out(p, u):
                sp.wait_ge(out_sb[p], u + 1)
                t = FIRST[p] + u
                for g in sorted({g for g, _ in QUADRANTS[t]}):
                    own = [(q, i) for q, (group, i) in enumerate(QUADRANTS[t]) if group == g]
                    (q0, i0), (q1, i1) = own[0], own[-1]
                    sp.dma_start(out[GB * g:GB * (g + 1), i0:i1 + 1, :].rearrange("b i n -> i b n"),
                                 ob[GB * q0:GB * (q1 + 1), u, :]).then_inc(dma_out, 16)

            pair(0)
            pair(1)
            for x in range(2):
                sp.wait_ge(wkq_lo[x], KT)
                block_load(A, x)
            pair(2)
            value_out(0)
            value_out(1)
            value_in(0)
            value_in(1)
            value_out(2)
            value_in(2)
            sp.wait_ge(wvo_lo, KT)
            block_load(A, 2)
            value_out(3)
            value_in(3)
            value_out(4)
            value_in(4)
            sp.wait_ge(wvo_lo, 2 * KT)
            block_load(A, 3)
            pair(3)
            pair(4)
            for i in range(SLOTS, NB):
                sp.wait_ge(wgu_lo[A], i - SLOTS + 1)
                sp.wait_ge(wd_lo[A], i - SLOTS + 1)
                block_load(A, i)
            for i in range(SLOTS):
                sp.wait_ge(wgu_lo[A], NB - SLOTS + i + 1)
                sp.wait_ge(wd_lo[A], NB - SLOTS + i + 1)
                block_load(BB, i)
            for u in range(TILES[A]):
                tile_out(A, u)
            with sp.Fori(0, NB // SLOTS - 1) as n:
                for u in range(SLOTS):
                    sp.wait_ge(wgu_lo[BB], SLOTS * n + (u + 1))
                    sp.wait_ge(wd_lo[BB], SLOTS * n + (u + 1))
                    sp.dma_start(stage[:, u, 0:FW], w_ffn[bass.ds(SLOTS * n + (SLOTS + u), 1)].rearrange("o p n -> (o p) n"))\
                      .then_inc(dma_stage[u], 16)

            for u in range(TILES[BB]):
                tile_out(BB, u)
            sp.wait_ge(dma_out, 16 * (NT + 1))

        @block.gpsimd
        def _(pool):
            def low(dst, src, hi, done):
                pool.tensor_tensor(dst, src, f32(hi), ALU.subtract).then_inc(done, 1)

            def lo_kq(x, k):
                pool.wait_ge(wkq_hi[x], k + 1)
                low(wkq[x][:, 1, k], stage[:, x, D * k:D * (k + 1)], wkq[x][:, 0, k], wkq_lo[x])

            def lo_vo(n, k):
                pool.wait_ge(wvo_hi, KT * n + k + 1)
                low(wvo[:, 1, k], stage[:, 2 + n, D * k:D * (k + 1)], wvo[:, 0, k], wvo_lo)

            def power(n):
                t = NORMS[n][1]
                pool.wait_ge(ln_mv, n + 1)
                pool.tensor_scalar(var[:, t], mv[:, t, 1:2], EPS, None, ALU.add).then_inc(ln_var, 1)
                pool.wait_ge(ln_var, n + 1)
                pool.tensor_tensor(rs0[:, t], var[:, t], neghalf[:, :], ALU.pow).then_inc(ln_pow, 1)

            def rotation_sum(n):
                pool.wait_ge(rot_read, n + 1)
                if n >= ROT:
                    pool.wait_ge(rot_gone[n % ROT], 64 * (n // ROT))
                pool.tensor_tensor(rot[:, n % ROT], rot_cos[:, n % 2], rot_sin[:, n % 2], ALU.add).then_inc(rot_sum, 1)

            def scores(g, i):
                rotated(pool, g, i)
                key_products(pool, g, i).then_inc(score_pool, 1)

            def values(g, i):
                pool.wait_ge(probs, 1 + [m[0] == g and i in range(*m[2]) for m in MASKED].index(True))
                values_arrived(pool, g)
                pool.wait_ge(score_sum, NPOS * g + i + 1)
                value_products(pool, g, i).then_inc(pv_pool, 1)

            def lo_gu(i):
                pool.wait_ge(wgu_hi[A], i + 1)
                low(wgu[:, i % 2, 1], stage[:, i % SLOTS, 0:2 * KT * P], wgu[:, i % 2, 0], wgu_lo[A])

            def lo_down(i, ring, slot, p=A):
                pool.wait_ge(wd_hi[p], i + 1)
                low(wd[:, ring, 1], stage[:, slot, 2 * KT * P:FW], wd[:, ring, 0], wd_lo[p])

            def lo_block(i):
                lo_gu(i)
                lo_down(i - 1, (i - 1) % 2, (i - 1) % SLOTS)

            pool.memset(neghalf[:, :], -0.5).then_inc(neghalf_set, 1)
            pool.wait_ge(neghalf_set, 1)
            power(0)
            lo_kq(0, 0)
            power(1)
            lo_kq(0, 1)
            lo_kq(0, 2)
            power(2)
            lo_kq(0, 3)
            for k in range(KT):
                lo_kq(1, k)
            for n in range(3):
                rotation_sum(n)
            power(3)
            rotation_sum(3)
            power(4)
            lo_vo(0, 0)
            rotation_sum(4)
            lo_vo(0, 1)
            rotation_sum(5)
            lo_vo(0, 2)
            lo_vo(0, 3)
            scores(0, 5)
            scores(0, 7)
            scores(0, 9)
            rotation_sum(6)
            for k in range(KT):
                lo_vo(1, k)
            values(0, 9)
            rotation_sum(7)
            rotation_sum(8)
            values(0, 8)
            rotation_sum(9)
            lo_gu(0)
            power(LN2[1])
            power(LN2[0])
            lo_gu(1)
            scores(1, 5)
            scores(1, 7)
            lo_down(0, 0, 0)
            for i in range(2, 12):
                lo_block(i)
            values(1, 8)
            values(1, 7)
            values(1, 4)
            lo_block(12)
            lo_block(13)
            power(LN2[2])
            power(LN2[4])
            lo_block(14)
            power(LN2[3])
            lo_block(15)
            lo_down(15, 1, 3)
            with pool.Fori(0, NB // SLOTS) as n:
                for u in range(SLOTS):
                    lo_down(SLOTS * n + u, u % 2, u, p=BB)

        @block.scalar
        def _(act):
            def split_hi(dst, src, done):
                act.activation(dst, src, ACT.Copy).then_inc(done, 1)

            def embedded(t):
                act.wait_ge(tok_mm, t + 1)
                act.activation(h[:, t], ps[:, t, :], ACT.Copy).then_inc(h_sb, 1)

            def hi_kq(x, k):
                act.wait_ge(dma_stage[x], 16)
                split_hi(wkq[x][:, 0, k], stage[:, x, D * k:D * (k + 1)], wkq_hi[x])

            def hi_vo(n):
                act.wait_ge(dma_stage[2 + n], 16)
                if n == 1:
                    act.wait_ge(project_mm, len(PROJECT))
                    act.wait_ge(wvo_lo, KT)
                for k in range(KT):
                    split_hi(wvo[:, 0, k], stage[:, 2 + n, D * k:D * (k + 1)], wvo_hi)

            def hi_xT(n):
                t = NORMS[n][1]
                act.wait_ge(xnT_mm, n + 1)
                split_hi(xT[:, 0, :, P * t:P * (t + 1)],
                         ps[:, ln_bank(n), :].rearrange("p (k n) -> p k n", k=KT), xT_hi)

            def values_out(t):
                n = PROJECT.index(("v", t))
                act.wait_ge(project_mm, n + 1)
                if t >= 2:
                    act.wait_ge(v_gone[t % 2], 64 * (t // 2))
                act.activation(v_out[:, t % 2], ps[:, PROJECT_BANK[n % len(PROJECT_BANK)], :], ACT.Copy).then_inc(v_sb, 1)

            def exponential(n):
                part = slice(*SOFTMAX[n][2])
                act.wait_ge(exp_in, n + 1)
                act.activation(pr[:, part], pr[:, part], ACT.Exp).then_inc(exp_out, 1)

            def hi_attn(u):
                act.wait_ge(pv_mm, VALUES.index((UNITS[u][0], UNITS[u][3][-1])) + 1)
                a, b = UNITS[u][2]
                split_hi(xT[:, 0, :, columns(u)],
                         ps[:, UNIT_BANK[u], :].rearrange("p (k n) -> p k n", k=KT)[:, :, GB * a:GB * b], attn_hi)

            def hi_gu(p, i, ring, slot):
                act.wait_ge(dma_stage[slot], stage_count(p, i, slot))
                split_hi(wgu[:, ring, 0], stage[:, slot, 0:2 * KT * P], wgu_hi[p])

            def hi_down(p, i, ring, slot):
                split_hi(wd[:, ring, 0], stage[:, slot, 2 * KT * P:FW], wd_hi[p])

            act.wait_ge(dma_pat, 16)
            split_hi(pat[:, 0], pat_raw[:, :], pat_hi)
            act.wait_ge(dma_tok, 16)
            split_hi(wtok[:, 0], wtok_raw[:, :], wtok_hi)
            act.wait_ge(dma_bias, 16)
            split_hi(bias[:, 0], bias_raw[:, :], bias_hi)
            embedded(0)
            embedded(1)
            hi_kq(0, 0)
            hi_kq(0, 1)
            embedded(2)
            hi_kq(0, 2)
            hi_kq(0, 3)
            embedded(3)
            hi_xT(0)
            embedded(4)
            hi_kq(1, 0)
            hi_kq(1, 1)
            hi_xT(1)
            hi_kq(1, 2)
            hi_kq(1, 3)
            hi_xT(2)
            hi_vo(0)
            hi_xT(3)
            hi_xT(4)
            for t in range(NT - 2):
                values_out(t)
            exponential(0)
            exponential(1)
            exponential(2)
            for t in range(NT - 2, NT):
                values_out(t)
            hi_vo(1)
            hi_gu(A, 0, 0, 0)
            hi_down(A, 0, 0, 0)
            hi_gu(A, 1, 1, 1)
            act.wait_ge(neghalf_set, 1)
            act.activation(warm[:, :], neghalf[:, :], ACT.Silu)
            hi_attn(0)
            hi_attn(1)
            hi_attn(2)
            hi_xT(LN2[1])
            hi_xT(LN2[0])

            def ffn_step(p, i, u, first=False, next_gu=True, next_down=True):
                ring = u % 2
                cols = slice(0, P * TILES[p])
                (gate, at) = GATE[p][ring]
                act.wait_ge(gu_mm[p], 2 * i + (2 if p == A else 1))
                act.activation(silu[:, ring, cols], ps[:, gate, at:at + P * TILES[p]], ACT.Silu).then_inc(silu_done[p], 1)
                if next_gu:
                    act.wait_ge(gu_mm[p], 2 * i + 2)
                    act.wait_ge(wgu_lo[p], i + 1)
                    hi_gu(p, i + 2, ring, (u + 2) % SLOTS)
                act.wait_ge(gu_prod[p], i + 1)
                if not first:
                    act.wait_ge(down_mm[p], i - 1)
                split_hi(hT[:, ring, 0, cols], gu[:, ring, cols], hT_hi[p])
                if next_down:
                    if not (isinstance(i, int) and i < 1):
                        act.wait_ge(down_mm[p], i)
                        act.wait_ge(wd_lo[p], i)
                    hi_down(p, i + 1, 1 - ring, (u + 1) % SLOTS)

            def first_pass(i):
                ffn_step(A, i, i % SLOTS, first=i < 2,
                         next_gu=i < NB - 2, next_down=i < NB - 1)

            rotation_done(act)
            for i in range(6):
                first_pass(i)
            exponential(3)
            for i in range(6, 9):
                first_pass(i)
            exponential(4)
            for i in range(9, 12):
                first_pass(i)
            hi_attn(3)
            hi_attn(4)
            first_pass(12)
            hi_attn(5)
            hi_xT(LN2[2])
            first_pass(13)
            hi_xT(LN2[4])
            first_pass(14)
            hi_xT(LN2[3])
            act.wait_ge(gu_mm[A], 2 * NB - 2)
            act.wait_ge(wgu_lo[A], NB - 1)
            hi_gu(BB, 0, 0, 0)
            first_pass(15)
            act.wait_ge(down_mm[A], NB - 1)
            act.wait_ge(wd_lo[A], NB - 1)
            hi_down(BB, 0, 0, 0)
            act.wait_ge(gu_mm[A], 2 * NB)
            act.wait_ge(wgu_lo[A], NB)
            hi_gu(BB, 1, 1, 1)
            act.wait_ge(down_mm[A], NB - 1 + TILES[A])

            ffn_step(BB, 0, 0, first=True)
            ffn_step(BB, 1, 1, first=True)
            with act.Fori(0, NB // SLOTS - 1) as n:
                for u in range(SLOTS):
                    ffn_step(BB, SLOTS * n + (u + 2), (u + 2) % SLOTS)
            ffn_step(BB, NB - 2, 2, next_gu=False)
            ffn_step(BB, NB - 1, 3, next_gu=False, next_down=False)

        @block.vector
        def _(dve):
            steps = [0]

            def step(ins):
                steps[0] += 1
                ins.then_inc(dve_step, 1)
                dve.wait_ge(dve_step, steps[0])

            def statistics(n):
                ln, t = NORMS[n]
                if ln == 0:
                    dve.wait_ge(h_sb, t + 1)
                else:
                    dve.wait_ge(wo_mm, WO.index(t) + 1)
                    step(dve.tensor_tensor(h[:, t], ps[:, WO_BANK[t], :], h[:, t], ALU.add))
                step(dve.bn_stats(stats[:, t], h[:, t]))
                dve.bn_aggr(mv[:, t], stats[:, t]).then_inc(ln_mv, 1)

            def normalise(n):
                t = NORMS[n][1]
                dve.wait_ge(ln_pow, n + 1)
                step(dve.tensor_scalar(rs1[:, t], var[:, t], rs0[:, t], rs0[:, t], ALU.mult, ALU.mult))
                step(dve.tensor_scalar(rs2[:, t], rs1[:, t], -0.5, 1.5, ALU.mult, ALU.add))
                step(dve.tensor_tensor(rstd[:, t], rs0[:, t], rs2[:, t], ALU.mult))
                if n >= 2:
                    dve.wait_ge(xnT_mm, n - 1)
                dve.tensor_scalar(xn[:, n % 2], h[:, t], mv[:, t, 0:1], rstd[:, t],
                                  ALU.subtract, ALU.mult).then_inc(xn_ready, 1)

            def low(n):
                t = NORMS[n][1]
                cols = slice(P * t, P * (t + 1))
                dve.wait_ge(xT_hi, n + 1)
                dve.tensor_tensor(xT[:, 1, :, cols], ps[:, ln_bank(n), :].rearrange("p (k n) -> p k n", k=KT),
                                  f32(xT[:, 0, :, cols]), ALU.subtract).then_inc(xT_lo, 1)

            def low_attn(u):
                a, b = UNITS[u][2]
                dve.wait_ge(attn_hi, u + 1)
                dve.tensor_tensor(xT[:, 1, :, columns(u)],
                                  ps[:, UNIT_BANK[u], :].rearrange("p (k n) -> p k n", k=KT)[:, :, GB * a:GB * b],
                                  f32(xT[:, 0, :, columns(u)]), ALU.subtract).then_inc(attn_lo, 1)

            def rotate(x, t):
                n, at = ROTATE.index((x, t)), PROJECT.index((x, t))
                dve.wait_ge(project_mm, at + 1)
                if n >= 2:
                    dve.wait_ge(rot_sum, n - 1)
                src = ps[:, PROJECT_BANK[at % len(PROJECT_BANK)], :].rearrange("p (h a d) -> p h a d", h=H, a=2)
                cos, sin = (cut[f + x][:, HD * t:HD * (t + 1)].rearrange("p (a d) -> p a d", a=2) for f in ("cos", "sin"))
                by_cos, by_sin = (f[:, n % 2].rearrange("p (h a d) -> p h a d", h=H, a=2) for f in (rot_cos, rot_sin))
                dve.tensor_tensor(by_cos, src, repeated(cos, 1, H), ALU.mult)
                for a in range(2):
                    last = dve.tensor_tensor(by_sin[:, :, a], src[:, :, 1 - a], repeated(sin[:, a], 1, H), ALU.mult)
                last.then_inc(rot_read, 1)

            def scores(g, i):
                if (g, i) in POOL_SCORES:
                    dve.wait_ge(score_pool, POOL_SCORES.index((g, i)) + 1)
                else:
                    rotated(dve, g, i)
                    step(key_products(dve, g, i))
                dve.tensor_reduce(sm[:, i, :, 0:i + 1].rearrange("p h j -> p j h"),
                                  products(i).rearrange("p j (h d) -> p j h d", d=HD),
                                  AX_X, ALU.add).then_inc(score_sum, 1)

            def rows(x, part):
                return x[:, slice(*part)].rearrange("p i h j -> p (i h) j")

            def softmax_in(n):
                g, masked, part = SOFTMAX[n]
                if masked:
                    mask(part)
                else:
                    dve.wait_ge(score_sum, NPOS * g + part[1])
                    if g:
                        dve.wait_ge(pv_pool, value_number((g - 1, 8)))
                flat = rowv[:, 0, slice(*part)].rearrange("p i h -> p (i h)")
                step(dve.tensor_reduce(flat, rows(sm, part), AX_X, ALU.max))
                step(dve.tensor_scalar(flat, flat, -BIG, None, ALU.max))
                dve.scalar_tensor_tensor(rows(pr, part), rows(sm, part), -BIG, repeated(flat, 2, NPOS),
                                         ALU.max, ALU.subtract).then_inc(exp_in, 1)

            def softmax_out(n):
                g, masked, part = SOFTMAX[n]
                dve.wait_ge(exp_out, n + 1)
                total, inverse = (rowv[:, x, slice(*part)].rearrange("p i h -> p (i h)") for x in range(2))
                step(dve.tensor_reduce(total, rows(pr, part), AX_X, ALU.add))
                step(dve.reciprocal(inverse, total))
                last = dve.tensor_tensor(rows(pr, part), rows(pr, part), repeated(inverse, 2, NPOS), ALU.mult)
                if masked:
                    last.then_inc(probs, 1)
                else:
                    step(last)

            def heavy_keys():
                flat = hvy[:, 0].rearrange("p h j -> p (h j)")
                step(dve.tensor_reduce(flat, pr[:, :, :, :].rearrange("p i h j -> p (h j) i"), AX_X, ALU.add))
                step(dve.tensor_reduce(hvm[:, 0], hvy[:, 0], AX_X, ALU.max))
                step(dve.tensor_tensor(hvy[:, 1], hvy[:, 0], repeated(hvm[:, 0], 2, NPOS), ALU.is_equal))
                step(dve.tensor_tensor(hvy[:, 0], hvy[:, 1], repeated(cut["rank"], 1, HQ), ALU.mult))
                step(dve.tensor_reduce(hvm[:, 1], hvy[:, 0], AX_X, ALU.max))
                step(dve.tensor_tensor(hvy[:, 1], hvy[:, 0], repeated(hvm[:, 1], 2, NPOS), ALU.is_equal))
                step(dve.tensor_scalar(hvy[:, 0], hvy[:, 1], 2.0, -1.0, ALU.mult, ALU.add))
                step(dve.tensor_scalar(hvy[:, 2], hvy[:, 0], BIG, None, ALU.mult))

            def mask(part):
                n = part[1] - part[0]
                band = cut["band"].rearrange("p (i j) -> p i j", j=NPOS)[:, slice(*part)]
                step(dve.tensor_tensor(keep[:, slice(*part)], repeated(hvy[:, 2], 1, n), repeated(band, 2, HQ), ALU.max))
                step(dve.tensor_tensor(rows(sm, part), rows(sm, part), rows(keep, part), ALU.min))

            def values(g, *queries):
                values_arrived(dve, g)
                for i in queries:
                    dve.wait_ge(probs, 1 + [m[0] == g and i in range(*m[2]) for m in MASKED].index(True))
                    value_products(dve, g, i).then_inc(pv_dve, 1)

            step(dve.memset(ones_raw[:, :], 1.0))
            dve.tensor_copy(ones[:, :], ones_raw[:, :]).then_inc(ones_set, 1)
            dve.wait_ge(pat_hi, 1)
            dve.tensor_tensor(pat[:, 1], pat_raw[:, :], f32(pat[:, 0]), ALU.subtract).then_inc(pat_lo, 1)
            dve.wait_ge(wtok_hi, 1)
            dve.tensor_tensor(wtok[:, 1], wtok_raw[:, :], f32(wtok[:, 0]), ALU.subtract).then_inc(wtok_lo, 1)
            dve.wait_ge(bias_hi, 1)
            dve.tensor_tensor(bias[:, 1], bias_raw[:, :], f32(bias[:, 0]), ALU.subtract).then_inc(bias_lo, 1)
            dve.memset(sm[:, :, :, :], -BIG)
            statistics(0)
            statistics(1)
            normalise(0)
            statistics(2)
            normalise(1)
            low(0)
            low(1)
            normalise(2)
            low(2)
            dve.wait_ge(dma_const, 16)
            rotate("k", 0)
            rotate("q", 0)
            rotate("k", 1)
            statistics(3)
            rotate("q", 1)
            statistics(4)
            normalise(3)
            rotate("k", 2)
            normalise(4)
            rotate("q", 2)
            for i in range(4):
                scores(0, i)
            low(3)
            low(4)
            for i in range(4, 8):
                scores(0, i)
            scores(0, 8)
            scores(0, 9)
            softmax_in(0)
            rotate("k", 3)
            softmax_out(0)
            heavy_keys()
            softmax_in(1)
            softmax_in(2)
            softmax_out(1)
            values(0, 7, 6)
            softmax_out(2)
            values(0, 5, 4, 3, 2, 1, 0)
            rotate("q", 3)
            rotate("k", 4)
            low_attn(0)
            low_attn(1)
            rotate("q", 4)
            statistics(LN2[1])
            statistics(LN2[0])
            normalise(LN2[1])
            normalise(LN2[0])
            low_attn(2)
            low(LN2[1])
            low(LN2[0])

            def lo_gu(p, i, ring, slot):
                dve.wait_ge(wgu_hi[p], i + 1)
                dve.tensor_tensor(wgu[:, ring, 1], stage[:, slot, 0:2 * KT * P], f32(wgu[:, ring, 0]), ALU.subtract)\
                   .then_inc(wgu_lo[p], 1)

            def up_product(p, i, ring):
                cols = slice(0, P * TILES[p])
                (up, at) = UP[p][ring]
                dve.wait_ge(gu_mm[p], 2 * i + 2)
                dve.wait_ge(silu_done[p], i + 1)
                dve.tensor_tensor(gu[:, ring, cols], silu[:, ring, cols], ps[:, up, at:at + P * TILES[p]], ALU.mult)\
                   .then_inc(gu_prod[p], 1)

            def low_product(p, i, ring):
                cols = slice(0, P * TILES[p])
                dve.wait_ge(hT_hi[p], i + 1)
                dve.tensor_tensor(hT[:, ring, 1, cols], gu[:, ring, cols], f32(hT[:, ring, 0, cols]),
                                  ALU.subtract).then_inc(hT_lo[p], 1)

            def first_pass(i):
                up_product(A, i, i % 2)
                low_product(A, i, i % 2)

            def second_pass(i, u, next_gu=True):
                up_product(BB, i, u % 2)
                low_product(BB, i, u % 2)
                if next_gu:
                    lo_gu(BB, i + 2, u % 2, (u + 2) % SLOTS)

            def tile_sum(p, u):
                dve.wait_ge(down_mm[p], NB + u)
                if p == BB and u < TILES[A]:
                    dve.wait_ge(dma_out, 16 * TILES[A])
                dve.tensor_tensor(ob[:, u], ps[:, DOWN[p][u], :], h[:, FIRST[p] + u], ALU.add).then_inc(out_sb[p], 1)

            for i in range(4):
                scores(1, i)
            rotation_done(dve)
            up_product(A, 0, 0)
            scores(1, 4)
            low_product(A, 0, 0)
            up_product(A, 1, 1)
            scores(1, 5)
            low_product(A, 1, 1)
            scores(1, 6)
            up_product(A, 2, 0)
            scores(1, 7)
            low_product(A, 2, 0)
            scores(1, 8)
            first_pass(3)
            scores(1, 9)
            first_pass(4)
            softmax_in(3)
            first_pass(5)
            up_product(A, 6, 0)
            softmax_out(3)
            low_product(A, 6, 0)
            heavy_keys()
            first_pass(7)
            softmax_in(4)
            first_pass(8)
            up_product(A, 9, 1)
            softmax_out(4)
            low_product(A, 9, 1)
            values(1, 9)
            up_product(A, 10, 0)
            values(1, 6)
            low_product(A, 10, 0)
            values(1, 5, 3)
            up_product(A, 11, 1)
            values(1, 2, 1)
            low_product(A, 11, 1)
            values(1, 0)
            low_attn(3)
            low_attn(4)
            first_pass(12)
            statistics(LN2[2])
            normalise(LN2[2])
            low_attn(5)
            statistics(LN2[4])
            first_pass(13)
            low(LN2[2])
            normalise(LN2[4])
            statistics(LN2[3])
            first_pass(14)
            low(LN2[4])
            normalise(LN2[3])
            low(LN2[3])
            lo_gu(BB, 0, 0, 0)
            first_pass(15)
            lo_gu(BB, 1, 1, 1)
            for u in range(TILES[A]):
                tile_sum(A, u)

            second_pass(0, 0)
            second_pass(1, 1)
            with dve.Fori(0, NB // SLOTS - 1) as n:
                for u in range(SLOTS):
                    second_pass(SLOTS * n + (u + 2), (u + 2) % SLOTS)
            second_pass(NB - 2, 2, next_gu=False)
            second_pass(NB - 1, 3, next_gu=False)
            for u in range(TILES[BB]):
                tile_sum(BB, u)

        @block.tensor
        def _(pe):
            pe.wait_ge(ones_set, 1)
            pe.wait_ge(wtok_hi, 1)

            def embed(t):
                tokens = [pat[:, a, P * t:P * (t + 1)] for a in range(2)]
                pe.matmul(ps[:, t, :], tokens[0], wtok[:, 0], start=True, stop=False)
                pe.wait_ge(pat_lo, 1)
                pe.matmul(ps[:, t, :], tokens[1], wtok[:, 0], start=False, stop=False)
                pe.wait_ge(wtok_lo, 1)
                pe.matmul(ps[:, t, :], tokens[0], wtok[:, 1], start=False, stop=False)
                pe.wait_ge(bias_lo, 1)
                pe.matmul(ps[:, t, :], ones[:, :], bias[:, 0], start=False, stop=False)
                pe.matmul(ps[:, t, :], ones[:, :], bias[:, 1], start=False, stop=True).then_inc(tok_mm, 1)

            def read_out(stage, n):
                if stage == "embedding":
                    pe.wait_ge(h_sb, n + 1)
                if stage == "projection":
                    x, t = n
                    if x == "v":
                        pe.wait_ge(v_sb, t + 1)
                    else:
                        pe.wait_ge(rot_read, ROTATE.index(n) + 1)
                if stage == "unit":
                    pe.wait_ge(attn_lo, n + 1)
                if stage == "wo":
                    pe.wait_ge(ln_mv, LN2[n] + 1)
                if stage == "norm":
                    pe.wait_ge(xT_lo, n + 1)

            def transposes(n, last):
                pe.wait_ge(xn_ready, n + 1)
                if last:
                    read_out(*last)
                for k in range(KT):
                    ins = pe.transpose(ps[:, ln_bank(n), P * k:P * (k + 1)], xn[:, n % 2, P * k:P * (k + 1)], cut["ident"])
                ins.then_inc(xnT_mm, 1)

            def project(n):
                x, t = PROJECT[n]
                w, low = (wvo, wvo_lo) if x == "v" else (wkq["kq".index(x)], wkq_lo["kq".index(x)])
                bank = PROJECT_BANK[n % len(PROJECT_BANK)]
                if n >= len(PROJECT_BANK):
                    read_out("projection", PROJECT[n - len(PROJECT_BANK)])
                elif bank < NT:
                    read_out("embedding", bank)
                pe.wait_ge(xT_lo, t + 1)
                for k in range(KT):
                    pe.wait_ge(low, k + 1)
                    ins = mm3(pe, ps[:, bank, :], [xT[:, a, k, P * t:P * (t + 1)] for a in range(2)],
                              [w[:, a, k] for a in range(2)], k == 0, k == KT - 1)
                ins.then_inc(project_mm, 1)

            def value_sums(u, last):
                g, t, (a, b), queries = UNITS[u]
                read_out(*last)
                for i in queries:
                    pe.wait_ge(pv_pool if (g, i) in POOL_VALUES else pv_dve, value_number((g, i)))
                    dst = ps[:, UNIT_BANK[u], :].rearrange("p (k q b) -> p k q b", k=KT, q=NQ)[:, :, QUADRANTS[t].index((g, i))]
                    for j in range(i + 1):
                        ins = pe.matmul(dst, products(i)[:, j], cut["ident"], start=j == 0, stop=j == i)
                    ins.then_inc(pv_mm, 1)

            def project_out(t, units, last):
                pe.wait_ge(wvo_lo, 2 * KT)
                pe.wait_ge(attn_lo, units)
                read_out(*last)
                for k in range(KT):
                    ins = mm3(pe, ps[:, WO_BANK[t], :], [xT[:, a, k, P * t:P * (t + 1)] for a in range(2)],
                              [wvo[:, a, k] for a in range(2)], k == 0, k == KT - 1)
                ins.then_inc(wo_mm, 1)

            for t in range(4):
                embed(t)
            pe.wait_ge(dma_const, 16)
            transposes(0, None)
            embed(4)
            transposes(1, None)
            project(0)
            transposes(2, ("norm", 0))
            for n in range(1, 6):
                project(n)
            transposes(3, ("norm", 1))
            transposes(4, ("norm", 2))
            for n in range(6, len(PROJECT)):
                project(n)
            value_sums(0, ("norm", 4))
            value_sums(1, ("norm", 3))
            project_out(1, 1, ("projection", ("v", 3)))
            project_out(0, 2, ("projection", ("v", 4)))
            value_sums(2, ("projection", ("k", 3)))
            transposes(LN2[1], ("unit", 0))
            transposes(LN2[0], ("unit", 1))

            def gate_up(p, i, ring):
                pe.wait_ge(wgu_lo[p], i + 1)
                at = P * FIRST[p]
                for up, (bank, col) in enumerate((GATE[p][ring], UP[p][ring])):
                    if p == BB and up and isinstance(i, int) and i == 1:
                        pe.wait_ge(out_sb[A], 1)
                    for k in range(KT):
                        w = D * up + P * k
                        ins = mm3(pe, ps[:, bank, col:col + P * TILES[p]], [wgu[:, ring, a, w:w + P] for a in range(2)],
                                  [xT[:, a, k, at:at + P * TILES[p]] for a in range(2)], k == 0, k == KT - 1)
                    ins.then_inc(gu_mm[p], 1)

            def down(p, i, ring, first=False, last=False):
                pe.wait_ge(hT_lo[p], i + 1)
                pe.wait_ge(wd_lo[p], i + 1)
                for u in range(TILES[p]):
                    ins = mm3(pe, ps[:, DOWN[p][u], :], [hT[:, ring, a, P * u:P * (u + 1)] for a in range(2)],
                              [wd[:, ring, a] for a in range(2)], first, last)
                    if last:
                        ins.then_inc(down_mm[p], 1)
                if not last:
                    ins.then_inc(down_mm[p], 1)

            def first_pass(i):
                if i < 2:
                    read_out("norm", LN2[0])
                else:
                    pe.wait_ge(gu_prod[A], i - 1)
                gate_up(A, i, i % 2)
                if i == 1:
                    read_out("wo", 0)
                if i > 0:
                    down(A, i - 1, (i - 1) % 2, first=i == 1)

            for i in range(12):
                first_pass(i)
            value_sums(3, ("projection", ("q", 3)))
            value_sums(4, ("projection", ("k", 4)))
            project_out(2, 4, ("projection", ("q", 4)))
            first_pass(12)
            value_sums(5, ("unit", 2))
            project_out(4, 5, ("unit", 3))
            transposes(LN2[2], ("unit", 4))
            first_pass(13)
            project_out(3, 6, ("wo", 2))
            transposes(LN2[4], ("unit", 5))
            first_pass(14)
            pe.wait_ge(gu_prod[A], NB - 2)
            gate_up(A, NB - 1, 1)
            transposes(LN2[3], ("wo", 4))
            down(A, NB - 2, 0)
            read_out("norm", LN2[3])
            pe.wait_ge(gu_prod[A], NB)
            gate_up(BB, 0, 0)
            down(A, NB - 1, 1, last=True)
            gate_up(BB, 1, 1)
            down(BB, 0, 0, first=True)
            with pe.Fori(0, NB // 2 - 1) as n:
                pe.wait_ge(gu_prod[BB], 2 * n + 1)
                gate_up(BB, 2 * n + 2, 0)
                down(BB, 2 * n + 1, 1)
                pe.wait_ge(gu_prod[BB], 2 * n + 2)
                gate_up(BB, 2 * n + 3, 1)
                down(BB, 2 * n + 2, 0)
            down(BB, NB - 1, 1, last=True)


def lay_out(x, L0_tok_W, L0_tok_b, L0_attn_Wq, L0_attn_Wk, L0_attn_Wv, L0_attn_Wo, L0_ffn_w_gate_up, L0_ffn_w_down):
    import numpy as np

    xs = np.asarray(x)[:, :, 0]
    patches = np.concatenate([xs[GB * g:GB * (g + 1), STRIDE * i:STRIDE * i + PATCH].T
                              for tile in QUADRANTS for g, i in tile], axis=1)

    def k_major(w):
        w = np.asarray(w)
        return w.T.reshape(-1, P, w.shape[0]).transpose(1, 0, 2)

    gate_up = k_major(L0_ffn_w_gate_up).reshape(P, KT, 2, NB, P).transpose(3, 0, 2, 1, 4).reshape(NB, P, 2 * KT * P)
    down = np.asarray(L0_ffn_w_down).T.reshape(NB, P, D)

    f = np.float32
    scale = f(1.0) / np.sqrt(f(HD))
    inv_freq = f(1.0) / f(10000.0) ** (np.arange(0, HD, 2, dtype=f) / f(HD))
    angle = (np.arange(NPOS, dtype=f)[:, None] * inv_freq[None, :]).astype(f)
    cos, sin = np.cos(angle).astype(f), np.sin(angle).astype(f)
    cos, sin = np.concatenate([cos, cos], axis=1), np.concatenate([-sin, sin], axis=1)
    rows = np.array([[i for _, i in tile] for tile in QUADRANTS]).T.repeat(GB, axis=0)
    by_tile = [table[rows].reshape(P, NT * HD) for table in (cos, sin, cos * scale, sin * scale)]
    pos = np.arange(NPOS)
    band = np.where(np.abs(pos[:, None] - pos[None, :]) <= 1, BIG, -BIG).reshape(-1)
    tables = dict(zip(("cosk", "sink", "cosq", "sinq"), by_tile), ident=np.eye(P),
                  band=np.tile(band, (P, 1)), rank=np.tile(NPOS - pos, (P, 1)))
    consts = np.concatenate([np.asarray(tables[n]).astype(f) for n in CUTS], axis=1)
    return {
        "patches": patches, "w_tok": np.asarray(L0_tok_W).T, "b_tok": np.asarray(L0_tok_b)[None, :],
        "w_k": k_major(L0_attn_Wk).reshape(P, KT * D), "w_q": k_major(L0_attn_Wq).reshape(P, KT * D),
        "w_v": k_major(L0_attn_Wv).reshape(P, KT * D), "w_o": k_major(L0_attn_Wo).reshape(P, KT * D),
        "w_ffn": np.concatenate([gate_up, down], axis=2), "consts": consts,
    }


def kernel(**inputs):
    import numpy as np
    from concourse import bacc
    from concourse.bass_utils import run_bass_kernel_spmd

    arrays = {n: np.ascontiguousarray(a) for n, a in lay_out(**inputs).items()}
    nc = bacc.Bacc("TRN2", target_bir_lowering=False, num_devices=1)
    args = [nc.dram_tensor(n, a.shape, F32, kind="ExternalInput").ap() for n, a in arrays.items()]
    out = nc.dram_tensor("out", (B, NPOS, D), F32, kind="ExternalOutput").ap()
    regroup = nc.dram_tensor("regroup", (3, NG, NQ, GB, NPOS, DH), F32, kind="Internal").ap()
    audio_tower(nc, *args, regroup, out)
    result = run_bass_kernel_spmd(nc, [arrays], core_ids=[0])
    return result.results[0]["out"]
```

```python
from contextlib import ExitStack

import concourse.bass as bass
from concourse import mybir

F32 = mybir.dt.float32
F32R = mybir.dt.float32r
ALU = mybir.AluOpType
ACT = mybir.ActivationFunctionType
AX_X = mybir.AxisListType.X

P = 128
B, SEQ = 64, 750
PATCH, STRIDE = 128, 64
NPOS = len(range(0, SEQ - PATCH + 1, STRIDE))
TOK = NPOS * B
NT = TOK // P
D, H, HD = 512, 16, 32
KT = D // P
NG, GB, NQ = 2, 32, 4
HQ = H // NQ
DH = HQ * HD
INTER = 2048
NB = INTER // P
FW = 2 * KT * P + D
BR = 32
EPS = 1e-5
BIG = 3.4028234663852886e38
CUTS = {"ident": P, "cosk": NT * HD, "sink": NT * HD, "cosq": NT * HD, "sinq": NT * HD,
        "band": NPOS * NPOS, "rank": NPOS}
CONSTS = sum(CUTS.values())
QUADRANTS = [[(0, n) for n in range(0, 4)], [(0, n) for n in range(4, 8)],
             [(g, n) for g in range(2) for n in (8, 9)],
             [(1, n) for n in range(0, 4)], [(1, n) for n in range(4, 8)]]

PROJECT = [("k", 0), ("q", 0), ("k", 1), ("q", 1), ("k", 2), ("q", 2), ("v", 0), ("v", 1), ("v", 2),
           ("k", 3), ("q", 3), ("k", 4), ("q", 4), ("v", 3), ("v", 4)]
ROTATE = [item for item in PROJECT if item[0] != "v"]
ROT = 4
NORMS = [(0, t) for t in range(NT)] + [(1, t) for t in (1, 0, 2, 4, 3)]
LN2 = {t: n for n, (ln, t) in enumerate(NORMS) if ln == 1}
UNITS = [(0, 1, (0, 4), (7, 6, 5, 4)), (0, 0, (0, 4), (3, 2, 1, 0)), (0, 2, (0, 2), (9, 8)),
         (1, 2, (2, 4), (9, 8)), (1, 4, (0, 4), (7, 6, 5, 4)), (1, 3, (0, 4), (3, 2, 1, 0))]
VALUES = [(unit[0], i) for unit in UNITS for i in unit[3]]
WO = [1, 0, 2, 4, 3]
POOL_SCORES = [(0, 5), (0, 7), (0, 9), (1, 5), (1, 7)]
POOL_VALUES = [(0, 9), (0, 8), (1, 8), (1, 7), (1, 4)]
SOFTMAX = [(0, 0, (0, 10)), (0, 1, (0, 8)), (0, 1, (8, 10)),
           (1, 0, (0, 10)), (1, 1, (0, 10))]
MASKED = [step for step in SOFTMAX if step[1] == 1]
LN1_BANK = [5, 6]
PROJECT_BANK = [7, 0, 1, 2, 3, 4]
UNIT_BANK = [5, 6, 2, 3, 4, 2]
WO_BANK = {1: 0, 0: 1, 2: 7, 4: 3, 3: 7}
LN2_BANK = {1: 5, 0: 6, 2: 4, 4: 2, 3: 3}
A, Z = 0, 1
FIRST, TILES = (0, 2), (2, 3)
GATE = (((5, 0), (6, 0)), ((5, 0), (7, 0)))
UP = (((5, 2 * P), (6, 2 * P)), ((6, 0), (0, 0)))
DOWN = ((0, 1), (2, 3, 4))
SLOTS = 4


def ln_bank(n):
    ln, t = NORMS[n]
    return LN2_BANK[t] if ln else LN1_BANK[n % 2]


def columns(unit):
    _, t, (a, b), _ = UNITS[unit]
    return slice(P * t + GB * a, P * t + GB * b)


def audio_tower(nc, patches, w_tok, b_tok, w_k, w_q, w_v, w_o, w_ffn, consts, regroup, out):
    ctx = ExitStack()
    with ctx:
        def sb(name, shape, dt=F32, stack=ctx):
            return stack.enter_context(nc.sbuf_tensor(name, shape, dt))

        def sem(name):
            return ctx.enter_context(nc.semaphore(name))

        def f32(ap):
            return ap.bitcast(F32)

        ps = ctx.enter_context(nc.psum_tensor("ps", [P, 8, 512], F32))

        const = sb("const", [P, CONSTS])
        at, cut = 0, {}
        for name, width in CUTS.items():
            cut[name] = const[:, at:at + width]
            at += width
        stage = sb("stage", [P, 4, 2048])
        wvo = sb("wvo", [P, 2, KT, D], F32R)
        xT = sb("xT", [P, 2, KT, TOK], F32R)
        h = sb("h", [P, NT, D])
        xn = sb("xn", [P, 2, D])
        stats = sb("stats", [P, NT, 6])
        mv = sb("mv", [P, NT, 2])
        var = sb("var", [P, NT, 1])
        neghalf = sb("neghalf", [P, 1])
        warm = sb("warm", [P, 1])
        rs0, rs1, rs2, rstd = (sb(n, [P, NT, 1]) for n in ("rs0", "rs1", "rs2", "rstd"))
        qk_mem = ExitStack()
        wkq = [sb(n, [P, 2, KT, D], F32R, qk_mem) for n in ("wk", "wq")]
        qk_mem.close()
        wgu = sb("wgu", [P, 2, 2, 2 * KT * P], F32R)
        wd = sb("wd", [P, 2, 2, D], F32R)
        ob = sb("ob", [P, 3, D])
        silu = sb("silu", [P, 2, 3 * P])
        rot_mem = ExitStack()
        rot_cos = sb("rot_cos", [P, 2, D], F32, rot_mem)
        rot_sin = sb("rot_sin", [P, 2, D], F32, rot_mem)
        rot = sb("rot", [P, ROT, D], F32, rot_mem)
        v_out = sb("v_out", [P, 2, D], F32, rot_mem)
        rot_mem.close()
        gu = sb("gu", [P, 2, 3 * P])
        hT = sb("hT", [P, 2, 2, 3 * P], F32R)
        sb("fill", [P, (4 + ROT + 2) * D - 6 * P - 12 * P])
        k_all, q_all, v_all = (sb(n, [P, NG, NPOS, DH]) for n in ("k_all", "q_all", "v_all"))
        embed_mem = ExitStack()
        pat_raw = sb("pat_raw", [P, TOK], F32, embed_mem)
        pat = sb("pat", [P, 2, TOK], F32R, embed_mem)
        wtok_raw = sb("wtok_raw", [P, D], F32, embed_mem)
        wtok = sb("wtok", [P, 2, D], F32R, embed_mem)
        bias_raw = sb("bias_raw", [2 * BR, D], F32, embed_mem)
        bias_hi = sb("bias_hi", [2 * BR, D], F32R, embed_mem)
        bias = sb("bias", [2 * BR, D], F32R, embed_mem)
        share_raw = sb("share_raw", [2 * BR, P], F32, embed_mem)
        share = sb("share", [2 * BR, P], F32R, embed_mem)
        embed_mem.close()
        prod = sb("prod", [P, NPOS * (NPOS + 1) // 2, DH])
        sm, pr, keep = (sb(n, [P, NPOS, HQ, NPOS]) for n in ("sm", "pr", "keep"))
        rowv = sb("rowv", [P, 2, NPOS, HQ])
        hvy = sb("hvy", [P, 3, HQ, NPOS])
        hvm = sb("hvm", [P, 2, HQ])

        dma_pat, dma_tok, dma_bias, dma_const = sem("dma_pat"), sem("dma_tok"), sem("dma_bias"), sem("dma_const")
        dma_stage = [sem(f"dma_stage{n}") for n in range(4)]
        rot_gone = [sem(f"rot_gone{n}") for n in range(ROT)]
        dma_kq = [sem(f"dma_kq{t}") for t in range(NT)]
        v_gone = [sem(f"v_gone{n}") for n in range(2)]
        dma_v = [sem(f"dma_v{g}") for g in range(NG)]
        dma_out = sem("dma_out")
        pat_hi, pat_lo, wtok_hi, wtok_lo = sem("pat_hi"), sem("pat_lo"), sem("wtok_hi"), sem("wtok_lo")
        wkq_hi, wkq_lo = [sem("wk_hi"), sem("wq_hi")], [sem("wk_lo"), sem("wq_lo")]
        wq_lo_late = sem("wq_lo_late")
        wvo_hi, wvo_lo = sem("wvo_hi"), sem("wvo_lo")
        share_set, neghalf_set = sem("share_set"), sem("neghalf_set")
        bias_high, bias_low = sem("bias_high"), sem("bias_low")
        tok_mm, h_sb, ln_mv, ln_var, ln_pow, xn_ready = (sem(n) for n in ("tok_mm", "h_sb", "ln_mv", "ln_var", "ln_pow", "xn_ready"))
        xnT_mm, xT_hi, xT_lo = sem("xnT_mm"), sem("xT_hi"), sem("xT_lo")
        project_mm, rot_read, rot_sum, v_sb = sem("project_mm"), sem("rot_read"), sem("rot_sum"), sem("v_sb")
        score_pool, score_sum = sem("score_pool"), sem("score_sum")
        exp_in, exp_out = sem("exp_in"), sem("exp_out")
        probs, pv_dve, pv_pool, pv_mm = sem("probs"), sem("pv_dve"), sem("pv_pool"), sem("pv_mm")
        attn_hi, attn_lo, wo_mm = sem("attn_hi"), sem("attn_lo"), sem("wo_mm")
        wgu_hi, wgu_lo, wd_hi, wd_lo, gu_mm, silu_done, gu_prod, hT_hi, hT_lo, down_mm, out_sb = (
            [sem(f"{n}_{p}") for p in "ab"] for n in
            ("wgu_hi", "wgu_lo", "wd_hi", "wd_lo", "gu_mm", "silu_done", "gu_prod", "hT_hi", "hT_lo", "down_mm", "out_sb"))
        dve_step = sem("dve_step")

        def repeated(ap, dim, n):
            ap = ap.unsqueeze(dim)
            return ap.broadcast_to([n if d == dim else size for d, size in enumerate(ap.shape)])

        def mm3(pe, dst, lhs, rhs, first, last):
            for n, (a, b) in enumerate(((0, 0), (0, 1), (1, 0))):
                ins = pe.matmul(dst, lhs[a], rhs[b], start=first and n == 0, stop=last and n == 2)
            return ins

        def rotated(eng, g, i):
            for t in ((0, 1, 2), (3, 4, 2))[g][:i // 4 + 1]:
                eng.wait_ge(dma_kq[t], 16 * 2 * len({group for group, _ in QUADRANTS[t]}))

        def values_arrived(eng, g):
            eng.wait_ge(dma_v[g], 16 * 3)

        def rotation_done(eng):
            for buffer in range(ROT):
                eng.wait_ge(rot_gone[buffer], 64 * len(range(buffer, len(ROTATE), ROT)))
            for buffer in range(2):
                eng.wait_ge(v_gone[buffer], 64 * len(range(buffer, NT, 2)))

        def products(i):
            return prod[:, i * (i + 1) // 2:(i + 1) * (i + 2) // 2]

        def kq_split(eng, x, k):
            if x == 1 and k >= KT - 2:
                eng.wait_ge(wkq_lo[1], KT - 2)
                eng.wait_ge(wq_lo_late, k - (KT - 3))
            else:
                eng.wait_ge(wkq_lo[x], k + 1)

        def key_products(eng, g, i):
            if g:
                eng.wait_ge(pv_mm, VALUES.index((g - 1, i)) + 1)
            return eng.tensor_tensor(products(i), repeated(q_all[:, g, i], 1, i + 1), k_all[:, g, 0:i + 1], ALU.mult)

        def value_products(eng, g, i):
            return eng.tensor_tensor(products(i).rearrange("p j (h d) -> p j h d", d=HD),
                                     v_all[:, g, 0:i + 1].rearrange("p j (h d) -> p j h d", d=HD),
                                     repeated(pr[:, i, :, 0:i + 1].rearrange("p h j -> p j h"), 3, HD), ALU.mult)

        def value_number(item):
            return sum((k in POOL_VALUES) == (item in POOL_VALUES) for k in VALUES[:VALUES.index(item) + 1])

        def stage_count(p, i, slot):
            before = 1 + p * NB // SLOTS
            return i * (16 // SLOTS) + (16 * (before + 1) - slot * (16 // SLOTS))

        block = ctx.enter_context(nc.Block())

        @block.sync
        def _(sp):
            sp.dma_start(pat_raw[:, :], patches).then_inc(dma_pat, 16)
            sp.dma_start(wtok_raw[:, :], w_tok).then_inc(dma_tok, 16)
            sp.dma_start(bias_raw[:, :], b_tok.broadcast_to([2 * BR, D])).then_inc(dma_bias, 16)
            sp.dma_start(stage[:, 0, :], w_k).then_inc(dma_stage[0], 16)
            sp.dma_start(const[:, :], consts).then_inc(dma_const, 16)
            sp.dma_start(stage[:, 1, :], w_q).then_inc(dma_stage[1], 16)
            sp.dma_start(stage[:, 2, :], w_v).then_inc(dma_stage[2], 16)
            sp.dma_start(stage[:, 3, :], w_o).then_inc(dma_stage[3], 16)

            def leave(x, t, buffer, done):
                for q, (g, i) in enumerate(QUADRANTS[t]):
                    sp.dma_start(regroup["kqv".index(x), g, :, :, i, :].rearrange("h b n -> b h n"),
                                 buffer[GB * q:GB * (q + 1)].rearrange("p (h n) -> p h n", h=NQ)).then_inc(done, 16)

            def enter(x, t, g, done):
                dst = {"k": k_all, "q": q_all, "v": v_all}[x]
                own = [i for group, i in QUADRANTS[t] if group == g]
                at = slice(own[0], own[-1] + 1)
                sp.dma_start(dst[:, g, at, :], regroup["kqv".index(x), g].rearrange("h b i n -> (h b) i n")[:, at, :])\
                  .then_inc(done, 16)

            def pair(t):
                items = [ROTATE.index((x, t)) for x in "kq"]
                for n in items:
                    sp.wait_ge(rot_sum, n + 1)
                    leave(ROTATE[n][0], t, rot[:, n % ROT], rot_gone[n % ROT])
                for n in items:
                    sp.wait_ge(rot_gone[n % ROT], 64 * (n // ROT + 1))
                    for g in sorted({g for g, _ in QUADRANTS[t]}):
                        enter(ROTATE[n][0], t, g, dma_kq[t])

            def value_out(t):
                sp.wait_ge(v_sb, t + 1)
                leave("v", t, v_out[:, t % 2], v_gone[t % 2])

            def value_in(t):
                sp.wait_ge(v_gone[t % 2], 64 * (t // 2 + 1))
                for g in sorted({g for g, _ in QUADRANTS[t]}):
                    enter("v", t, g, dma_v[g])

            def block_load(i):
                slot = i % SLOTS
                sp.dma_start(stage[:, slot, 0:FW], w_ffn[i]).then_inc(dma_stage[slot], 16)

            def tile_out(p, u):
                sp.wait_ge(out_sb[p], u + 1)
                t = FIRST[p] + u
                for g in sorted({g for g, _ in QUADRANTS[t]}):
                    own = [(q, i) for q, (group, i) in enumerate(QUADRANTS[t]) if group == g]
                    (q0, i0), (q1, i1) = own[0], own[-1]
                    sp.dma_start(out[GB * g:GB * (g + 1), i0:i1 + 1, :].rearrange("b i n -> i b n"),
                                 ob[GB * q0:GB * (q1 + 1), u, :]).then_inc(dma_out, 16)

            pair(0)
            pair(1)
            for x in range(2):
                kq_split(sp, x, KT - 1)
                block_load(x)
            pair(2)
            value_out(0)
            value_out(1)
            value_in(0)
            value_in(1)
            value_out(2)
            value_in(2)
            sp.wait_ge(wvo_lo, KT)
            block_load(2)
            value_out(3)
            value_in(3)
            value_out(4)
            value_in(4)
            sp.wait_ge(wvo_lo, 2 * KT)
            block_load(3)
            pair(3)
            pair(4)
            with sp.Fori(0, NB // SLOTS - 1) as n:
                for u in range(SLOTS):
                    sp.wait_ge(wgu_lo[A], SLOTS * n + (u + 1))
                    sp.wait_ge(wd_lo[A], SLOTS * n + (u + 1))
                    sp.dma_start(stage[:, u, 0:FW], w_ffn[bass.ds(SLOTS * n + (SLOTS + u), 1)].rearrange("o p n -> (o p) n"))\
                      .then_inc(dma_stage[u], 16)
            for i in range(SLOTS):
                sp.wait_ge(wgu_lo[A], NB - SLOTS + i + 1)
                sp.wait_ge(wd_lo[A], NB - SLOTS + i + 1)
                block_load(i)
            for u in range(TILES[A]):
                tile_out(A, u)
            with sp.Fori(0, NB // SLOTS - 1) as n:
                for u in range(SLOTS):
                    sp.wait_ge(wgu_lo[Z], SLOTS * n + (u + 1))
                    sp.wait_ge(wd_lo[Z], SLOTS * n + (u + 1))
                    sp.dma_start(stage[:, u, 0:FW], w_ffn[bass.ds(SLOTS * n + (SLOTS + u), 1)].rearrange("o p n -> (o p) n"))\
                      .then_inc(dma_stage[u], 16)

            for u in range(TILES[Z]):
                tile_out(Z, u)
            sp.wait_ge(dma_out, 16 * (NT + 1))

        @block.gpsimd
        def _(pool):
            def low(dst, src, hi, done):
                pool.tensor_tensor(dst, src, f32(hi), ALU.subtract).then_inc(done, 1)

            def lo_kq(x, k):
                pool.wait_ge(wkq_hi[x], k + 1)
                low(wkq[x][:, 1, k], stage[:, x, D * k:D * (k + 1)], wkq[x][:, 0, k], wkq_lo[x])

            def lo_vo(n, k):
                pool.wait_ge(wvo_hi, KT * n + k + 1)
                low(wvo[:, 1, k], stage[:, 2 + n, D * k:D * (k + 1)], wvo[:, 0, k], wvo_lo)

            def power(n):
                t = NORMS[n][1]
                pool.wait_ge(ln_mv, n + 1)
                pool.tensor_scalar(var[:, t], mv[:, t, 1:2], EPS, None, ALU.add).then_inc(ln_var, 1)
                pool.wait_ge(ln_var, n + 1)
                pool.tensor_tensor(rs0[:, t], var[:, t], neghalf[:, :], ALU.pow).then_inc(ln_pow, 1)

            def rotation_sum(n):
                pool.wait_ge(rot_read, n + 1)
                if n >= ROT:
                    pool.wait_ge(rot_gone[n % ROT], 64 * (n // ROT))
                pool.tensor_tensor(rot[:, n % ROT], rot_cos[:, n % 2], rot_sin[:, n % 2], ALU.add).then_inc(rot_sum, 1)

            def scores(g, i):
                rotated(pool, g, i)
                key_products(pool, g, i).then_inc(score_pool, 1)

            def values(g, i):
                pool.wait_ge(probs, 1 + [m[0] == g and i in range(*m[2]) for m in MASKED].index(True))
                values_arrived(pool, g)
                pool.wait_ge(score_sum, NPOS * g + i + 1)
                value_products(pool, g, i).then_inc(pv_pool, 1)

            def lo_gu(i, slot):
                pool.wait_ge(wgu_hi[A], i + 1)
                low(wgu[:, slot % 2, 1], stage[:, slot, 0:2 * KT * P], wgu[:, slot % 2, 0], wgu_lo[A])

            def lo_down(i, ring, slot, p=A):
                pool.wait_ge(wd_hi[p], i + 1)
                low(wd[:, ring, 1], stage[:, slot, 2 * KT * P:FW], wd[:, ring, 0], wd_lo[p])

            def lo_block(i, slot):
                lo_gu(i, slot)
                lo_down(i - 1, (slot + 1) % 2, (slot - 1) % SLOTS)

            pool.memset(neghalf[:, :], -0.5).then_inc(neghalf_set, 1)
            pool.wait_ge(neghalf_set, 1)
            power(0)
            lo_kq(0, 0)
            power(1)
            lo_kq(0, 1)
            lo_kq(0, 2)
            power(2)
            lo_kq(0, 3)
            for k in range(KT - 2):
                lo_kq(1, k)
            for n in range(3):
                rotation_sum(n)
            power(3)
            rotation_sum(3)
            power(4)
            lo_vo(0, 0)
            rotation_sum(4)
            lo_vo(0, 1)
            rotation_sum(5)
            lo_vo(0, 2)
            lo_vo(0, 3)
            scores(0, 5)
            scores(0, 7)
            scores(0, 9)
            rotation_sum(6)
            for k in range(KT):
                lo_vo(1, k)
            values(0, 9)
            rotation_sum(7)
            rotation_sum(8)
            values(0, 8)
            rotation_sum(9)
            lo_gu(0, 0)
            power(LN2[1])
            power(LN2[0])
            lo_gu(1, 1)
            lo_down(0, 0, 0)
            scores(1, 5)
            scores(1, 7)
            lo_block(2, 2)
            lo_block(3, 3)
            with pool.Fori(0, 2) as n:
                for u in range(SLOTS):
                    lo_block(SLOTS * n + (SLOTS + u), u)
            values(1, 8)
            values(1, 7)
            values(1, 4)
            lo_block(12, 0)
            lo_block(13, 1)
            power(LN2[2])
            power(LN2[4])
            lo_block(14, 2)
            power(LN2[3])
            lo_block(15, 3)
            lo_down(15, 1, 3)
            with pool.Fori(0, NB // SLOTS) as n:
                for u in range(SLOTS):
                    lo_down(SLOTS * n + u, u % 2, u, p=Z)

        @block.scalar
        def _(act):
            def split_hi(dst, src, done):
                act.activation(dst, src, ACT.Copy).then_inc(done, 1)

            def embedded(t):
                act.wait_ge(tok_mm, t + 1)
                act.activation(h[:, t], ps[:, t, :], ACT.Copy).then_inc(h_sb, 1)

            def hi_kq(x, k):
                act.wait_ge(dma_stage[x], 16)
                split_hi(wkq[x][:, 0, k], stage[:, x, D * k:D * (k + 1)], wkq_hi[x])

            def hi_vo(n):
                act.wait_ge(dma_stage[2 + n], 16)
                if n == 1:
                    act.wait_ge(project_mm, len(PROJECT))
                    act.wait_ge(wvo_lo, KT)
                for k in range(KT):
                    split_hi(wvo[:, 0, k], stage[:, 2 + n, D * k:D * (k + 1)], wvo_hi)

            def hi_xT(n):
                t = NORMS[n][1]
                act.wait_ge(xnT_mm, n + 1)
                split_hi(xT[:, 0, :, P * t:P * (t + 1)],
                         ps[:, ln_bank(n), :].rearrange("p (k n) -> p k n", k=KT), xT_hi)

            def values_out(t):
                n = PROJECT.index(("v", t))
                act.wait_ge(project_mm, n + 1)
                if t >= 2:
                    act.wait_ge(v_gone[t % 2], 64 * (t // 2))
                act.activation(v_out[:, t % 2], ps[:, PROJECT_BANK[n % len(PROJECT_BANK)], :], ACT.Copy).then_inc(v_sb, 1)

            def exponential(n):
                part = slice(*SOFTMAX[n][2])
                act.wait_ge(exp_in, n + 1)
                act.activation(pr[:, part], pr[:, part], ACT.Exp).then_inc(exp_out, 1)

            def hi_attn(u):
                act.wait_ge(pv_mm, VALUES.index((UNITS[u][0], UNITS[u][3][-1])) + 1)
                a, b = UNITS[u][2]
                split_hi(xT[:, 0, :, columns(u)],
                         ps[:, UNIT_BANK[u], :].rearrange("p (k n) -> p k n", k=KT)[:, :, GB * a:GB * b], attn_hi)

            def hi_gu(p, i, ring, slot):
                act.wait_ge(dma_stage[slot], stage_count(p, i, slot))
                split_hi(wgu[:, ring, 0], stage[:, slot, 0:2 * KT * P], wgu_hi[p])

            def hi_down(p, i, ring, slot):
                split_hi(wd[:, ring, 0], stage[:, slot, 2 * KT * P:FW], wd_hi[p])

            act.wait_ge(dma_pat, 16)
            split_hi(pat[:, 0], pat_raw[:, :], pat_hi)
            act.wait_ge(dma_tok, 16)
            split_hi(wtok[:, 0], wtok_raw[:, :], wtok_hi)
            act.wait_ge(dma_bias, 16)
            split_hi(bias_hi[:, :], bias_raw[:, :], bias_high)
            embedded(0)
            embedded(1)
            hi_kq(0, 0)
            hi_kq(0, 1)
            embedded(2)
            hi_kq(0, 2)
            hi_kq(0, 3)
            embedded(3)
            hi_xT(0)
            embedded(4)
            hi_kq(1, 0)
            hi_kq(1, 1)
            hi_xT(1)
            hi_kq(1, 2)
            hi_kq(1, 3)
            hi_xT(2)
            hi_vo(0)
            hi_xT(3)
            hi_xT(4)
            for t in range(NT - 2):
                values_out(t)
            exponential(0)
            exponential(1)
            exponential(2)
            for t in range(NT - 2, NT):
                values_out(t)
            hi_vo(1)
            hi_gu(A, 0, 0, 0)
            hi_down(A, 0, 0, 0)
            hi_gu(A, 1, 1, 1)
            act.wait_ge(neghalf_set, 1)
            act.activation(warm[:, :], neghalf[:, :], ACT.Silu)
            hi_attn(0)
            hi_attn(1)
            hi_attn(2)
            hi_xT(LN2[1])
            hi_xT(LN2[0])

            def ffn_step(p, i, u, first=False, next_gu=True, next_down=True):
                ring = u % 2
                cols = slice(0, P * TILES[p])
                (gate, at) = GATE[p][ring]
                act.wait_ge(gu_mm[p], 2 * i + (2 if p == A else 1))
                act.activation(silu[:, ring, cols], ps[:, gate, at:at + P * TILES[p]], ACT.Silu).then_inc(silu_done[p], 1)
                if next_gu:
                    act.wait_ge(gu_mm[p], 2 * i + 2)
                    act.wait_ge(wgu_lo[p], i + 1)
                    hi_gu(p, i + 2, ring, (u + 2) % SLOTS)
                act.wait_ge(gu_prod[p], i + 1)
                if not first:
                    act.wait_ge(down_mm[p], i - 1)
                split_hi(hT[:, ring, 0, cols], gu[:, ring, cols], hT_hi[p])
                if next_down:
                    if not (isinstance(i, int) and i < 1):
                        act.wait_ge(down_mm[p], i)
                        act.wait_ge(wd_lo[p], i)
                    hi_down(p, i + 1, 1 - ring, (u + 1) % SLOTS)

            def first_pass(i):
                ffn_step(A, i, i % SLOTS, first=i < 2,
                         next_gu=i < NB - 2, next_down=i < NB - 1)

            rotation_done(act)
            for i in range(6):
                first_pass(i)
            exponential(3)
            for i in range(6, 9):
                first_pass(i)
            exponential(4)
            for i in range(9, 12):
                first_pass(i)
            hi_attn(3)
            hi_attn(4)
            first_pass(12)
            hi_attn(5)
            hi_xT(LN2[2])
            first_pass(13)
            hi_xT(LN2[4])
            first_pass(14)
            act.wait_ge(gu_mm[A], 2 * NB - 2)
            act.wait_ge(wgu_lo[A], NB - 1)
            hi_gu(Z, 0, 0, 0)
            hi_xT(LN2[3])
            first_pass(15)
            act.wait_ge(down_mm[A], NB - 1)
            act.wait_ge(wd_lo[A], NB - 1)
            hi_down(Z, 0, 0, 0)
            act.wait_ge(gu_mm[A], 2 * NB)
            act.wait_ge(wgu_lo[A], NB)
            hi_gu(Z, 1, 1, 1)
            act.wait_ge(down_mm[A], NB - 1 + TILES[A])

            ffn_step(Z, 0, 0, first=True)
            ffn_step(Z, 1, 1, first=True)
            with act.Fori(0, NB // SLOTS - 1) as n:
                for u in range(SLOTS):
                    ffn_step(Z, SLOTS * n + (u + 2), (u + 2) % SLOTS)
            ffn_step(Z, NB - 2, 2, next_gu=False)
            ffn_step(Z, NB - 1, 3, next_gu=False, next_down=False)

        @block.vector
        def _(dve):
            steps = [0]

            def step(ins):
                steps[0] += 1
                ins.then_inc(dve_step, 1)
                dve.wait_ge(dve_step, steps[0])

            def statistics(n):
                ln, t = NORMS[n]
                if ln == 0:
                    dve.wait_ge(h_sb, t + 1)
                else:
                    dve.wait_ge(wo_mm, WO.index(t) + 1)
                    step(dve.tensor_tensor(h[:, t], ps[:, WO_BANK[t], :], h[:, t], ALU.add))
                step(dve.bn_stats(stats[:, t], h[:, t]))
                dve.bn_aggr(mv[:, t], stats[:, t]).then_inc(ln_mv, 1)

            def normalise(n):
                t = NORMS[n][1]
                dve.wait_ge(ln_pow, n + 1)
                step(dve.tensor_scalar(rs1[:, t], var[:, t], rs0[:, t], rs0[:, t], ALU.mult, ALU.mult))
                step(dve.tensor_scalar(rs2[:, t], rs1[:, t], -0.5, 1.5, ALU.mult, ALU.add))
                step(dve.tensor_tensor(rstd[:, t], rs0[:, t], rs2[:, t], ALU.mult))
                if n >= 2:
                    dve.wait_ge(xnT_mm, n - 1)
                dve.tensor_scalar(xn[:, n % 2], h[:, t], mv[:, t, 0:1], rstd[:, t],
                                  ALU.subtract, ALU.mult).then_inc(xn_ready, 1)

            def low(n):
                t = NORMS[n][1]
                cols = slice(P * t, P * (t + 1))
                dve.wait_ge(xT_hi, n + 1)
                dve.tensor_tensor(xT[:, 1, :, cols], ps[:, ln_bank(n), :].rearrange("p (k n) -> p k n", k=KT),
                                  f32(xT[:, 0, :, cols]), ALU.subtract).then_inc(xT_lo, 1)

            def low_attn(u):
                a, b = UNITS[u][2]
                dve.wait_ge(attn_hi, u + 1)
                dve.tensor_tensor(xT[:, 1, :, columns(u)],
                                  ps[:, UNIT_BANK[u], :].rearrange("p (k n) -> p k n", k=KT)[:, :, GB * a:GB * b],
                                  f32(xT[:, 0, :, columns(u)]), ALU.subtract).then_inc(attn_lo, 1)

            def rotate(x, t):
                n, at = ROTATE.index((x, t)), PROJECT.index((x, t))
                dve.wait_ge(project_mm, at + 1)
                if n >= 2:
                    dve.wait_ge(rot_sum, n - 1)
                src = ps[:, PROJECT_BANK[at % len(PROJECT_BANK)], :].rearrange("p (h a d) -> p h a d", h=H, a=2)
                cos, sin = (cut[f + x][:, HD * t:HD * (t + 1)].rearrange("p (a d) -> p a d", a=2) for f in ("cos", "sin"))
                by_cos, by_sin = (f[:, n % 2].rearrange("p (h a d) -> p h a d", h=H, a=2) for f in (rot_cos, rot_sin))
                dve.tensor_tensor(by_cos, src, repeated(cos, 1, H), ALU.mult)
                for a in range(2):
                    last = dve.tensor_tensor(by_sin[:, :, a], src[:, :, 1 - a], repeated(sin[:, a], 1, H), ALU.mult)
                last.then_inc(rot_read, 1)

            def scores(g, i):
                if (g, i) in POOL_SCORES:
                    dve.wait_ge(score_pool, POOL_SCORES.index((g, i)) + 1)
                else:
                    rotated(dve, g, i)
                    step(key_products(dve, g, i))
                dve.tensor_reduce(sm[:, i, :, 0:i + 1].rearrange("p h j -> p j h"),
                                  products(i).rearrange("p j (h d) -> p j h d", d=HD),
                                  AX_X, ALU.add).then_inc(score_sum, 1)

            def rows(x, part):
                return x[:, slice(*part)].rearrange("p i h j -> p (i h) j")

            def softmax_in(n):
                g, masked, part = SOFTMAX[n]
                if masked:
                    mask(part)
                else:
                    dve.wait_ge(score_sum, NPOS * g + part[1])
                    if g:
                        dve.wait_ge(pv_pool, value_number((g - 1, 8)))
                flat = rowv[:, 0, slice(*part)].rearrange("p i h -> p (i h)")
                step(dve.tensor_reduce(flat, rows(sm, part), AX_X, ALU.max))
                step(dve.tensor_scalar(flat, flat, -BIG, None, ALU.max))
                dve.scalar_tensor_tensor(rows(pr, part), rows(sm, part), -BIG, repeated(flat, 2, NPOS),
                                         ALU.max, ALU.subtract).then_inc(exp_in, 1)

            def softmax_out(n):
                g, masked, part = SOFTMAX[n]
                dve.wait_ge(exp_out, n + 1)
                total, inverse = (rowv[:, x, slice(*part)].rearrange("p i h -> p (i h)") for x in range(2))
                step(dve.tensor_reduce(total, rows(pr, part), AX_X, ALU.add))
                step(dve.reciprocal(inverse, total))
                last = dve.tensor_tensor(rows(pr, part), rows(pr, part), repeated(inverse, 2, NPOS), ALU.mult)
                if masked:
                    last.then_inc(probs, 1)
                else:
                    step(last)

            def heavy_keys():
                flat = hvy[:, 0].rearrange("p h j -> p (h j)")
                step(dve.tensor_reduce(flat, pr[:, :, :, :].rearrange("p i h j -> p (h j) i"), AX_X, ALU.add))
                step(dve.tensor_reduce(hvm[:, 0], hvy[:, 0], AX_X, ALU.max))
                step(dve.tensor_tensor(hvy[:, 1], hvy[:, 0], repeated(hvm[:, 0], 2, NPOS), ALU.is_equal))
                step(dve.tensor_tensor(hvy[:, 0], hvy[:, 1], repeated(cut["rank"], 1, HQ), ALU.mult))
                step(dve.tensor_reduce(hvm[:, 1], hvy[:, 0], AX_X, ALU.max))
                step(dve.tensor_tensor(hvy[:, 1], hvy[:, 0], repeated(hvm[:, 1], 2, NPOS), ALU.is_equal))
                step(dve.tensor_scalar(hvy[:, 0], hvy[:, 1], 2.0, -1.0, ALU.mult, ALU.add))
                step(dve.tensor_scalar(hvy[:, 2], hvy[:, 0], BIG, None, ALU.mult))

            def mask(part):
                n = part[1] - part[0]
                band = cut["band"].rearrange("p (i j) -> p i j", j=NPOS)[:, slice(*part)]
                step(dve.tensor_tensor(keep[:, slice(*part)], repeated(hvy[:, 2], 1, n), repeated(band, 2, HQ), ALU.max))
                step(dve.tensor_tensor(rows(sm, part), rows(sm, part), rows(keep, part), ALU.min))

            def values(g, *queries):
                values_arrived(dve, g)
                for i in queries:
                    dve.wait_ge(probs, 1 + [m[0] == g and i in range(*m[2]) for m in MASKED].index(True))
                    value_products(dve, g, i).then_inc(pv_dve, 1)

            step(dve.memset(share_raw[:, :], 1 / BR))
            dve.tensor_copy(share[:, :], share_raw[:, :]).then_inc(share_set, 1)
            dve.wait_ge(pat_hi, 1)
            dve.tensor_tensor(pat[:, 1], pat_raw[:, :], f32(pat[:, 0]), ALU.subtract).then_inc(pat_lo, 1)
            dve.wait_ge(wtok_hi, 1)
            dve.tensor_tensor(wtok[:, 1], wtok_raw[:, :], f32(wtok[:, 0]), ALU.subtract).then_inc(wtok_lo, 1)
            dve.wait_ge(bias_high, 1)
            dve.tensor_copy(bias[0:BR], f32(bias_hi[0:BR])).then_inc(bias_low, 1)
            dve.tensor_tensor(bias[BR:2 * BR], bias_raw[BR:2 * BR], f32(bias_hi[BR:2 * BR]), ALU.subtract)\
               .then_inc(bias_low, 1)
            dve.memset(sm[:, :, :, :], -BIG)
            statistics(0)
            statistics(1)
            normalise(0)
            statistics(2)
            normalise(1)
            low(0)
            low(1)
            normalise(2)
            for k in range(KT - 2, KT):
                dve.wait_ge(wkq_hi[1], k + 1)
                dve.tensor_tensor(wkq[1][:, 1, k], stage[:, 1, D * k:D * (k + 1)], f32(wkq[1][:, 0, k]), ALU.subtract)\
                   .then_inc(wq_lo_late, 1)
            low(2)
            dve.wait_ge(dma_const, 16)
            rotate("k", 0)
            rotate("q", 0)
            rotate("k", 1)
            statistics(3)
            rotate("q", 1)
            statistics(4)
            normalise(3)
            rotate("k", 2)
            normalise(4)
            rotate("q", 2)
            for i in range(4):
                scores(0, i)
            low(3)
            low(4)
            for i in range(4, 8):
                scores(0, i)
            scores(0, 8)
            scores(0, 9)
            softmax_in(0)
            rotate("k", 3)
            softmax_out(0)
            heavy_keys()
            softmax_in(1)
            softmax_in(2)
            softmax_out(1)
            values(0, 7, 6)
            softmax_out(2)
            values(0, 5, 4, 3, 2, 1, 0)
            rotate("q", 3)
            rotate("k", 4)
            rotate("q", 4)
            low_attn(0)
            low_attn(1)
            statistics(LN2[1])
            statistics(LN2[0])
            normalise(LN2[1])
            normalise(LN2[0])
            low_attn(2)
            low(LN2[1])
            low(LN2[0])

            def lo_gu(p, i, ring, slot):
                dve.wait_ge(wgu_hi[p], i + 1)
                dve.tensor_tensor(wgu[:, ring, 1], stage[:, slot, 0:2 * KT * P], f32(wgu[:, ring, 0]), ALU.subtract)\
                   .then_inc(wgu_lo[p], 1)

            def up_product(p, i, ring):
                cols = slice(0, P * TILES[p])
                (up, at) = UP[p][ring]
                dve.wait_ge(gu_mm[p], 2 * i + 2)
                dve.wait_ge(silu_done[p], i + 1)
                dve.tensor_tensor(gu[:, ring, cols], silu[:, ring, cols], ps[:, up, at:at + P * TILES[p]], ALU.mult)\
                   .then_inc(gu_prod[p], 1)

            def low_product(p, i, ring):
                cols = slice(0, P * TILES[p])
                dve.wait_ge(hT_hi[p], i + 1)
                dve.tensor_tensor(hT[:, ring, 1, cols], gu[:, ring, cols], f32(hT[:, ring, 0, cols]),
                                  ALU.subtract).then_inc(hT_lo[p], 1)

            def first_pass(i):
                up_product(A, i, i % 2)
                low_product(A, i, i % 2)

            def second_pass(i, u, next_gu=True):
                up_product(Z, i, u % 2)
                low_product(Z, i, u % 2)
                if next_gu:
                    lo_gu(Z, i + 2, u % 2, (u + 2) % SLOTS)

            def tile_sum(p, u):
                dve.wait_ge(down_mm[p], NB + u)
                if p == Z and u < TILES[A]:
                    dve.wait_ge(dma_out, 16 * TILES[A])
                dve.tensor_tensor(ob[:, u], ps[:, DOWN[p][u], :], h[:, FIRST[p] + u], ALU.add).then_inc(out_sb[p], 1)

            for i in range(4):
                scores(1, i)
            rotation_done(dve)
            up_product(A, 0, 0)
            scores(1, 4)
            low_product(A, 0, 0)
            up_product(A, 1, 1)
            scores(1, 5)
            low_product(A, 1, 1)
            scores(1, 6)
            up_product(A, 2, 0)
            scores(1, 7)
            low_product(A, 2, 0)
            scores(1, 8)
            first_pass(3)
            scores(1, 9)
            first_pass(4)
            softmax_in(3)
            first_pass(5)
            up_product(A, 6, 0)
            softmax_out(3)
            low_product(A, 6, 0)
            heavy_keys()
            first_pass(7)
            softmax_in(4)
            first_pass(8)
            up_product(A, 9, 1)
            softmax_out(4)
            low_product(A, 9, 1)
            values(1, 9)
            up_product(A, 10, 0)
            values(1, 6)
            low_product(A, 10, 0)
            values(1, 5, 3)
            up_product(A, 11, 1)
            values(1, 2, 1)
            low_product(A, 11, 1)
            values(1, 0)
            low_attn(3)
            low_attn(4)
            first_pass(12)
            statistics(LN2[2])
            normalise(LN2[2])
            low_attn(5)
            statistics(LN2[4])
            first_pass(13)
            low(LN2[2])
            normalise(LN2[4])
            statistics(LN2[3])
            first_pass(14)
            low(LN2[4])
            normalise(LN2[3])
            lo_gu(Z, 0, 0, 0)
            low(LN2[3])
            first_pass(15)
            lo_gu(Z, 1, 1, 1)
            for u in range(TILES[A]):
                tile_sum(A, u)

            second_pass(0, 0)
            second_pass(1, 1)
            with dve.Fori(0, NB // SLOTS - 1) as n:
                for u in range(SLOTS):
                    second_pass(SLOTS * n + (u + 2), (u + 2) % SLOTS)
            second_pass(NB - 2, 2, next_gu=False)
            second_pass(NB - 1, 3, next_gu=False)
            for u in range(TILES[Z]):
                tile_sum(Z, u)

        @block.tensor
        def _(pe):
            pe.wait_ge(share_set, 1)
            pe.wait_ge(wtok_hi, 1)

            def embed(t):
                tokens = [pat[:, a, P * t:P * (t + 1)] for a in range(2)]
                pe.matmul(ps[:, t, :], tokens[0], wtok[:, 0], start=True, stop=False)
                pe.wait_ge(pat_lo, 1)
                pe.matmul(ps[:, t, :], tokens[1], wtok[:, 0], start=False, stop=False)
                pe.wait_ge(wtok_lo, 1)
                pe.matmul(ps[:, t, :], tokens[0], wtok[:, 1], start=False, stop=False)
                pe.wait_ge(bias_low, 2)
                pe.matmul(ps[:, t, :], share[:, :], bias[:, :], start=False, stop=True).then_inc(tok_mm, 1)

            def read_out(stage, n):
                if stage == "embedding":
                    pe.wait_ge(h_sb, n + 1)
                if stage == "projection":
                    x, t = n
                    if x == "v":
                        pe.wait_ge(v_sb, t + 1)
                    else:
                        pe.wait_ge(rot_read, ROTATE.index(n) + 1)
                if stage == "unit":
                    pe.wait_ge(attn_lo, n + 1)
                if stage == "wo":
                    pe.wait_ge(ln_mv, LN2[n] + 1)
                if stage == "norm":
                    pe.wait_ge(xT_lo, n + 1)

            def transposes(n, last):
                pe.wait_ge(xn_ready, n + 1)
                if last:
                    read_out(*last)
                for k in range(KT):
                    ins = pe.transpose(ps[:, ln_bank(n), P * k:P * (k + 1)], xn[:, n % 2, P * k:P * (k + 1)], cut["ident"])
                ins.then_inc(xnT_mm, 1)

            def project(n):
                x, t = PROJECT[n]
                w = wvo if x == "v" else wkq["kq".index(x)]
                bank = PROJECT_BANK[n % len(PROJECT_BANK)]
                if n >= len(PROJECT_BANK):
                    read_out("projection", PROJECT[n - len(PROJECT_BANK)])
                elif bank < NT:
                    read_out("embedding", bank)
                pe.wait_ge(xT_lo, t + 1)
                for k in range(KT):
                    if x == "v":
                        pe.wait_ge(wvo_lo, k + 1)
                    else:
                        kq_split(pe, "kq".index(x), k)
                    ins = mm3(pe, ps[:, bank, :], [xT[:, a, k, P * t:P * (t + 1)] for a in range(2)],
                              [w[:, a, k] for a in range(2)], k == 0, k == KT - 1)
                ins.then_inc(project_mm, 1)

            def value_sums(u, last):
                g, t, (a, b), queries = UNITS[u]
                read_out(*last)
                for i in queries:
                    pe.wait_ge(pv_pool if (g, i) in POOL_VALUES else pv_dve, value_number((g, i)))
                    dst = ps[:, UNIT_BANK[u], :].rearrange("p (k q b) -> p k q b", k=KT, q=NQ)[:, :, QUADRANTS[t].index((g, i))]
                    for j in range(i + 1):
                        ins = pe.matmul(dst, products(i)[:, j], cut["ident"], start=j == 0, stop=j == i)
                    ins.then_inc(pv_mm, 1)

            def project_out(t, units, last):
                pe.wait_ge(wvo_lo, 2 * KT)
                pe.wait_ge(attn_lo, units)
                read_out(*last)
                for k in range(KT):
                    ins = mm3(pe, ps[:, WO_BANK[t], :], [xT[:, a, k, P * t:P * (t + 1)] for a in range(2)],
                              [wvo[:, a, k] for a in range(2)], k == 0, k == KT - 1)
                ins.then_inc(wo_mm, 1)

            for t in range(4):
                embed(t)
            pe.wait_ge(dma_const, 16)
            transposes(0, None)
            embed(4)
            transposes(1, None)
            project(0)
            transposes(2, ("norm", 0))
            for n in range(1, 6):
                project(n)
            transposes(3, ("norm", 1))
            transposes(4, ("norm", 2))
            for n in range(6, len(PROJECT)):
                project(n)
            value_sums(0, ("norm", 4))
            value_sums(1, ("norm", 3))
            project_out(1, 1, ("projection", ("v", 3)))
            project_out(0, 2, ("projection", ("v", 4)))
            value_sums(2, ("projection", ("k", 3)))
            transposes(LN2[1], ("unit", 0))
            transposes(LN2[0], ("unit", 1))

            def gate_up(p, i, ring):
                pe.wait_ge(wgu_lo[p], i + 1)
                at = P * FIRST[p]
                for up, (bank, col) in enumerate((GATE[p][ring], UP[p][ring])):
                    if p == Z and up and isinstance(i, int) and i == 1:
                        pe.wait_ge(out_sb[A], 1)
                    for k in range(KT):
                        w = D * up + P * k
                        ins = mm3(pe, ps[:, bank, col:col + P * TILES[p]], [wgu[:, ring, a, w:w + P] for a in range(2)],
                                  [xT[:, a, k, at:at + P * TILES[p]] for a in range(2)], k == 0, k == KT - 1)
                    ins.then_inc(gu_mm[p], 1)

            def down(p, i, ring, first=False, last=False):
                pe.wait_ge(hT_lo[p], i + 1)
                pe.wait_ge(wd_lo[p], i + 1)
                for u in range(TILES[p]):
                    ins = mm3(pe, ps[:, DOWN[p][u], :], [hT[:, ring, a, P * u:P * (u + 1)] for a in range(2)],
                              [wd[:, ring, a] for a in range(2)], first, last)
                    if last:
                        ins.then_inc(down_mm[p], 1)
                if not last:
                    ins.then_inc(down_mm[p], 1)

            def first_pass(i, ring):
                pe.wait_ge(gu_prod[A], i - 1)
                gate_up(A, i, ring)
                down(A, i - 1, 1 - ring)

            read_out("norm", LN2[0])
            gate_up(A, 0, 0)
            gate_up(A, 1, 1)
            read_out("wo", 0)
            down(A, 0, 0, first=True)
            with pe.Fori(0, 5) as n:
                first_pass(2 * n + 2, 0)
                first_pass(2 * n + 3, 1)
            value_sums(3, ("projection", ("q", 3)))
            value_sums(4, ("projection", ("k", 4)))
            project_out(2, 4, ("projection", ("q", 4)))
            first_pass(12, 0)
            value_sums(5, ("unit", 2))
            project_out(4, 5, ("unit", 3))
            transposes(LN2[2], ("unit", 4))
            first_pass(13, 1)
            project_out(3, 6, ("wo", 2))
            transposes(LN2[4], ("unit", 5))
            first_pass(14, 0)
            pe.wait_ge(gu_prod[A], NB - 2)
            gate_up(A, NB - 1, 1)
            transposes(LN2[3], ("wo", 4))
            down(A, NB - 2, 0)
            read_out("norm", LN2[3])
            pe.wait_ge(gu_prod[A], NB)
            gate_up(Z, 0, 0)
            down(A, NB - 1, 1, last=True)
            gate_up(Z, 1, 1)
            down(Z, 0, 0, first=True)
            with pe.Fori(0, NB // 2 - 1) as n:
                pe.wait_ge(gu_prod[Z], 2 * n + 1)
                gate_up(Z, 2 * n + 2, 0)
                down(Z, 2 * n + 1, 1)
                pe.wait_ge(gu_prod[Z], 2 * n + 2)
                gate_up(Z, 2 * n + 3, 1)
                down(Z, 2 * n + 2, 0)
            down(Z, NB - 1, 1, last=True)


def lay_out(x, L0_tok_W, L0_tok_b, L0_attn_Wq, L0_attn_Wk, L0_attn_Wv, L0_attn_Wo, L0_ffn_w_gate_up, L0_ffn_w_down):
    import numpy as np

    xs = np.asarray(x)[:, :, 0]
    patches = np.concatenate([xs[GB * g:GB * (g + 1), STRIDE * i:STRIDE * i + PATCH].T
                              for tile in QUADRANTS for g, i in tile], axis=1)

    def k_major(w):
        w = np.asarray(w)
        return w.T.reshape(-1, P, w.shape[0]).transpose(1, 0, 2)

    gate_up = k_major(L0_ffn_w_gate_up).reshape(P, KT, 2, NB, P).transpose(3, 0, 2, 1, 4).reshape(NB, P, 2 * KT * P)
    down = np.asarray(L0_ffn_w_down).T.reshape(NB, P, D)

    f = np.float32
    scale = f(1.0) / np.sqrt(f(HD))
    inv_freq = f(1.0) / f(10000.0) ** (np.arange(0, HD, 2, dtype=f) / f(HD))
    angle = (np.arange(NPOS, dtype=f)[:, None] * inv_freq[None, :]).astype(f)
    cos, sin = np.cos(angle).astype(f), np.sin(angle).astype(f)
    cos, sin = np.concatenate([cos, cos], axis=1), np.concatenate([-sin, sin], axis=1)
    rows = np.array([[i for _, i in tile] for tile in QUADRANTS]).T.repeat(GB, axis=0)
    by_tile = [table[rows].reshape(P, NT * HD) for table in (cos, sin, cos * scale, sin * scale)]
    pos = np.arange(NPOS)
    band = np.where(np.abs(pos[:, None] - pos[None, :]) <= 1, BIG, -BIG).reshape(-1)
    tables = dict(zip(("cosk", "sink", "cosq", "sinq"), by_tile), ident=np.eye(P),
                  band=np.tile(band, (P, 1)), rank=np.tile(NPOS - pos, (P, 1)))
    consts = np.concatenate([np.asarray(tables[n]).astype(f) for n in CUTS], axis=1)
    return {
        "patches": patches, "w_tok": np.asarray(L0_tok_W).T, "b_tok": np.asarray(L0_tok_b)[None, :],
        "w_k": k_major(L0_attn_Wk).reshape(P, KT * D), "w_q": k_major(L0_attn_Wq).reshape(P, KT * D),
        "w_v": k_major(L0_attn_Wv).reshape(P, KT * D), "w_o": k_major(L0_attn_Wo).reshape(P, KT * D),
        "w_ffn": np.concatenate([gate_up, down], axis=2), "consts": consts,
    }


def kernel(**inputs):
    import numpy as np
    from concourse import bacc
    from concourse.bass_utils import run_bass_kernel_spmd

    arrays = {n: np.ascontiguousarray(a) for n, a in lay_out(**inputs).items()}
    nc = bacc.Bacc("TRN2", target_bir_lowering=False, num_devices=1)
    args = [nc.dram_tensor(n, a.shape, F32, kind="ExternalInput").ap() for n, a in arrays.items()]
    out = nc.dram_tensor("out", (B, NPOS, D), F32, kind="ExternalOutput").ap()
    regroup = nc.dram_tensor("regroup", (3, NG, NQ, GB, NPOS, DH), F32, kind="Internal").ap()
    audio_tower(nc, *args, regroup, out)
    result = run_bass_kernel_spmd(nc, [arrays], core_ids=[0])
    return result.results[0]["out"]
```
